# Optimizing a Trainium2 kernel written in Bass

```python
import numpy as np
import jax
import jax.numpy as jnp

def _softmax(x, axis=-1):
    return jax.nn.softmax(x, axis=axis)

def _gelu(x):
    return jax.nn.gelu(x, approximate=True)

def _silu(x):
    return jax.nn.silu(x)

def _sigmoid(x):
    return jax.nn.sigmoid(x)

def _layernorm(x, axis=-1, eps=1e-05):
    m = jnp.mean(x, axis=axis, keepdims=True)
    v = jnp.var(x, axis=axis, keepdims=True)
    return (x - m) / jnp.sqrt(v + eps)

def _scatter_add(tgt, idx, src, axis=0):
    return tgt.at[idx].add(src)

def _segment_sum(src, seg, n):
    return jax.ops.segment_sum(src, seg, n)
kernel_name = 'mk_seq_postln_d1_jaxref_r8_45ca34'

def setup_inputs(seed: int=0):
    np.random.seed(seed)
    _w = jnp.asarray

    def _L0_attn_setup():
        import jax, jax.numpy as jnp
        import numpy as np
        D_MODEL = 128
        NUM_HEADS = 16
        D_HEAD = D_MODEL // NUM_HEADS
        LAMBDA_INIT = 0.8
        EPS = 1e-05
        B, N = (4, 128)
        key = jax.random.key(seed)
        ks = jax.random.split(key, 10)
        w_scale = 1.0 / np.sqrt(D_MODEL)
        d2 = 2 * D_HEAD * NUM_HEADS
        return {'X': jax.random.normal(ks[0], (B, N, D_MODEL), jnp.float32), 'Wq': jax.random.normal(ks[1], (d2, D_MODEL), jnp.float32) * w_scale, 'Wk': jax.random.normal(ks[2], (d2, D_MODEL), jnp.float32) * w_scale, 'Wv': jax.random.normal(ks[3], (d2, D_MODEL), jnp.float32) * w_scale, 'Wo': jax.random.normal(ks[4], (D_MODEL, d2), jnp.float32) * w_scale, 'lq1': jax.random.normal(ks[5], (NUM_HEADS, D_HEAD), jnp.float32), 'lk1': jax.random.normal(ks[6], (NUM_HEADS, D_HEAD), jnp.float32), 'lq2': jax.random.normal(ks[7], (NUM_HEADS, D_HEAD), jnp.float32), 'lk2': jax.random.normal(ks[8], (NUM_HEADS, D_HEAD), jnp.float32), 'rms_scale': jnp.ones((2 * D_HEAD,), jnp.float32)}
    _L0_attn_in = _L0_attn_setup()

    def _L0_ffn_setup():
        import jax, jax.numpy as jnp
        import numpy as np
        key = jax.random.key(seed)
        k0, k1, k2, k3 = jax.random.split(key, 4)
        B, S, D, F, E = (8, 256, 128, 256, 8)
        x = jax.random.normal(k0, (B, S, D), dtype=jnp.float32)
        Wg = jax.random.normal(k1, (D, E), dtype=jnp.float32) * 0.02
        W1 = jax.random.normal(k2, (E, D, F), dtype=jnp.float32) * 0.02
        W2 = jax.random.normal(k3, (E, F, D), dtype=jnp.float32) * 0.02
        return {'x': x, 'Wg': Wg, 'W1': W1, 'W2': W2}
    _L0_ffn_in = _L0_ffn_setup()
    _d = {'L0_attn_X': _L0_attn_in['X'], 'L0_attn_Wq': _L0_attn_in['Wq'], 'L0_attn_Wk': _L0_attn_in['Wk'], 'L0_attn_Wv': _L0_attn_in['Wv'], 'L0_attn_Wo': _L0_attn_in['Wo'], 'L0_attn_lq1': _L0_attn_in['lq1'], 'L0_attn_lk1': _L0_attn_in['lk1'], 'L0_attn_lq2': _L0_attn_in['lq2'], 'L0_attn_lk2': _L0_attn_in['lk2'], 'L0_attn_rms_scale': _L0_attn_in['rms_scale'], 'L0_ffn_Wg': _L0_ffn_in['Wg'], 'L0_ffn_W1': _L0_ffn_in['W1'], 'L0_ffn_W2': _L0_ffn_in['W2']}
    _x0 = _d['L0_attn_X']
    _d['L0_attn_X'] = jax.random.normal(jax.random.fold_in(jax.random.key(seed), 1), (2, 1024, 128), dtype=_x0.dtype)
    del _x0
    return _d

def reference(L0_attn_X, L0_attn_Wq, L0_attn_Wk, L0_attn_Wv, L0_attn_Wo, L0_attn_lq1, L0_attn_lk1, L0_attn_lq2, L0_attn_lk2, L0_attn_rms_scale, L0_ffn_Wg, L0_ffn_W1, L0_ffn_W2):

    def _L0_attn_ref(X, Wq, Wk, Wv, Wo, lq1, lk1, lq2, lk2, rms_scale):
        import jax, jax.numpy as jnp
        import numpy as np
        D_MODEL = 128
        NUM_HEADS = 16
        D_HEAD = D_MODEL // NUM_HEADS
        LAMBDA_INIT = 0.8
        EPS = 1e-05
        B, N = (4, 128)
        b, n, _ = X.shape
        H, dh = (NUM_HEADS, D_HEAD)

        def proj(W):
            return (X @ W.T).reshape(b, n, H, 2 * dh).transpose(0, 2, 1, 3)
        Q, K, V = (proj(Wq), proj(Wk), proj(Wv))
        Q1, Q2 = jnp.split(Q, 2, axis=-1)
        K1, K2 = jnp.split(K, 2, axis=-1)
        lam = jnp.exp(jnp.sum(lq1 * lk1, axis=-1)) - jnp.exp(jnp.sum(lq2 * lk2, axis=-1)) + LAMBDA_INIT
        lam = lam[None, :, None, None]
        scaling = 1.0 / np.sqrt(dh)
        causal = jnp.tril(jnp.ones((n, n), bool))
        A1 = jnp.where(causal, jnp.einsum('bhnd,bhmd->bhnm', Q1, K1) * scaling, -jnp.inf)
        A2 = jnp.where(causal, jnp.einsum('bhnd,bhmd->bhnm', Q2, K2) * scaling, -jnp.inf)
        attn = jax.nn.softmax(A1, axis=-1) - lam * jax.nn.softmax(A2, axis=-1)
        O = jnp.einsum('bhnm,bhmd->bhnd', attn, V)
        rms = jnp.sqrt(jnp.mean(O * O, axis=-1, keepdims=True) + EPS)
        O = O / rms * rms_scale * (1.0 - LAMBDA_INIT)
        Oc = O.transpose(0, 2, 1, 3).reshape(b, n, H * 2 * dh)
        return Oc @ Wo.T

    def _L0_ffn_ref(x, Wg, W1, W2):
        import jax, jax.numpy as jnp
        import numpy as np
        B, S, D = x.shape
        E = Wg.shape[1]
        T = B * S
        cap = max(1, T // E)
        xt = x.reshape(T, D)
        logits = xt @ Wg
        probs = jax.nn.softmax(logits, axis=-1)
        pT = probs.T
        _, top_idx = jax.lax.top_k(pT, cap)
        sel = jnp.zeros((E, T), dtype=bool).at[jnp.arange(E)[:, None], top_idx].set(True)
        masked = jnp.where(sel, pT, -jnp.inf)
        assigned = sel.any(axis=0)
        tok2exp = jnp.where(assigned, jnp.argmax(masked, axis=0), jnp.argmax(pT, axis=0))
        weights = jnp.take_along_axis(probs, tok2exp[:, None], axis=1)[:, 0]
        out = jnp.zeros_like(xt)
        for e in range(E):
            gate = jnp.where(tok2exp == e, weights, 0.0)
            h = jax.nn.gelu(xt @ W1[e], approximate=False) @ W2[e]
            out = out + gate[:, None] * h
        return out.reshape(B, S, D)
    x = L0_attn_X
    x = _layernorm(x + _L0_attn_ref(x, L0_attn_Wq, L0_attn_Wk, L0_attn_Wv, L0_attn_Wo, L0_attn_lq1, L0_attn_lk1, L0_attn_lq2, L0_attn_lk2, L0_attn_rms_scale), axis=-1)
    x = _layernorm(x + _L0_ffn_ref(x, L0_ffn_Wg, L0_ffn_W1, L0_ffn_W2), axis=-1)
    return x

_drawn_inputs = setup_inputs


def setup_inputs(seed=0):
    import zlib

    import numpy as np

    out = dict(_drawn_inputs(seed))
    spreads = {'L0_attn_rms_scale': (1.0, 0.2)}
    factors = {'L0_ffn_Wg': 8.0, 'L0_ffn_W1': 8.0, 'L0_ffn_W2': 8.0}
    for name, (base, spread) in spreads.items():
        noise = np.random.default_rng([zlib.crc32(name.encode()), seed]).standard_normal(out[name].shape)
        drawn = base * np.exp(spread * noise) if base else spread * noise
        out[name] = jnp.asarray(drawn.astype(out[name].dtype))
    for name, factor in factors.items():
        out[name] = (out[name] * factor).astype(out[name].dtype)
    return out
```

```python
from contextlib import ExitStack

import concourse.bass as bass
from concourse import mybir

ALU = mybir.AluOpType
ACT = mybir.ActivationFunctionType
AX = mybir.AxisListType
F32 = mybir.dt.float32
BF16 = mybir.dt.bfloat16
I32 = mybir.dt.int32

B, N, D = 2, 1024, 128
H, DH = 16, 8
E, F = 8, 256
T = B * N
CAP = T // E
LAMBDA_INIT, EPS = 0.8, 1e-5
SCALE = float(DH) ** -0.5

P = 128
BANK = 512
NT = N // P
TT = T // P
MAPS = 4
GB = 2 * H // MAPS
G = B * GB
ROWS = 9 * DH
SROWS = ROWS + 2
NBUF = 3
NRING = 3
NSLOT = 3
UNROLL = NBUF
LOOPS = (G - 1) // UNROLL

MAX_TILES = [[7], [6, 0], [5, 1], [4, 2], [3], [], [], []]
O_STEP = 2
M_STEP = 6


def spans(lo, hi):
    out = []
    while lo < hi:
        end = min(hi, (lo // BANK + 1) * BANK)
        out.append((lo, end))
        lo = end
    return out


SCORE_UNITS = [[(c, a, z) for c in range(MAPS) for a, z in spans(P * j, N)] for j in range(NT)]
MAX_UNITS = [[(c, i, n, a, z) for i in step for c in range(MAPS) for n, (a, z) in enumerate(spans(0, P * (i + 1)))]
             for step in MAX_TILES]
SCORES_BEFORE = [sum(map(len, SCORE_UNITS[:s])) for s in range(NT + 1)]
N_SCORES = SCORES_BEFORE[-1]
N_MAXIMA = sum(map(len, MAX_UNITS))
FIRST_A = N_MAXIMA + 1
N_A = N_MAXIMA + 1 + 2
assert N_SCORES % NRING == 0 and N_A % NRING == 0 and (UNROLL * NT) % NSLOT == 0


SPLIT_STEP = max(s for s in range(NT) if MAX_TILES[s])
LOAD_INC = 6 * 16
N_SMALL = 4 + P // (2 * DH) + 9
N_BITS = 30


def interleave(x, y):
    out, i, j = [], 0, 0
    while i < len(x) or j < len(y):
        if j >= len(y) or (i < len(x) and i * len(y) <= j * len(x)):
            out.append(x[i])
            i += 1
        else:
            out.append(y[j])
            j += 1
    return out


def a_items(step, last):
    items = [] if last else [("max", u) for u in MAX_UNITS[step]]
    if step == O_STEP:
        items += [("out", 0), ("out", 1)]
    if step == M_STEP and not last:
        items += [("shift", None)]
    return items


A_OUT_DONE = sum(len(a_items(s, False)) for s in range(O_STEP + 1))


def build(nc, X, XT, WqT, WkT, WvT, WoT, lq1, lk1, lq2, lk2, rms, Wg, W1, W2, c_ident, c_causal, c_same, c_before, out):
    parts_dram = nc.dram_tensor("parts", (2, 3, G * MAPS * DH, N), BF16).ap()

    ctx = ExitStack()
    with ctx:
        def sb(name, shape, dt=F32):
            return ctx.enter_context(nc.sbuf_tensor(name, shape, dt))

        def sem(name):
            return ctx.enter_context(nc.semaphore(name))

        x_tok = sb("x_tok", [P, TT, D])
        xT = sb("xT", [P, T])
        wq, wk, wv = (sb(n, [P, 2 * DH * H]) for n in ("wq", "wk", "wv"))
        wo = sb("wo", [P, 2, D])
        wg = sb("wg", [P, E])
        w1 = sb("w1", [P, E, F])
        w2 = sb("w2", [P, E, 2, D])
        ident = sb("ident", [P, P])
        identb = sb("identb", [P, P], BF16)
        causalf = sb("causalf", [P, P])
        causalb = sb("causalb", [P, P], BF16)
        same = sb("same", [P, P])
        before = sb("before", [P, P])
        lvec = sb("lvec", [P, 4, H, DH])
        lprod = sb("lprod", [P, 2, H, DH])
        lsum = sb("lsum", [P, 2, H])
        lexp = sb("lexp", [P, 2, H])
        nlam = sb("nlam", [P, G + 1, 2])
        rmscol = sb("rmscol", [P, 1])
        arena = sb("arena", [P, 6 * 4096])
        HT_SLOTS = 6
        a_b = arena[:, :].bitcast(BF16)
        nq = MAPS * N
        q_op = [a_b[:, u * nq:(u + 1) * nq].rearrange("p (c n) -> p c n", c=MAPS) for u in range(NBUF)]
        k_op = [a_b[:, (NBUF + u) * nq:(NBUF + u + 1) * nq].rearrange("p (c n) -> p c n", c=MAPS) for u in range(NBUF)]
        p_at = NBUF * nq
        probs = [arena[:, p_at + s * nq:p_at + (s + 1) * nq].rearrange("p (c n) -> p c n", c=MAPS) for s in range(NSLOT)]
        pa = 2 * p_at
        part_sb = [a_b[:, pa + u * 3 * BANK:pa + (u + 1) * 3 * BANK].rearrange("p (r n) -> p r n", r=3) for u in range(16)]
        hT = [arena[:, s * 4096:(s + 1) * 4096].rearrange("p (f n) -> p f n", f=2) for s in range(HT_SLOTS)]
        rest = sb("rest", [P, 2, BANK])
        v_all = sb("v_all", [P, G, 2, NT, 2 * DH])
        v_grp = sb("v_grp", [P, NBUF, 2, NT, 32])
        oT = sb("oT", [P, N])
        o_all = sb("o_all", [P, G + 1, NT, 2, 2 * DH])
        rinv = sb("rinv", [P, 2, 4, MAPS])
        o_norm = sb("o_norm", [P, 2, 4, MAPS, 2 * DH])
        m_raw = sb("m_raw", [P, MAPS, NT, 2])
        m_neg = sb("m_neg", [P, MAPS * NT])
        m_parts = sb("m_parts", [P, 4, MAPS * NT], BF16)
        mT = sb("mT", [2 * MAPS * NT, P], BF16)
        ss = sb("ss", [P, G * NT * 2])
        stats = sb("stats", [P, TT, 6])
        mv = sb("mv", [P, TT, 2])
        rstd = sb("rstd", [P, TT])
        ocT = sb("ocT", [P, 2, 2, D])
        lg = sb("lg", [P, TT, E])
        pr = sb("pr", [P, TT, E])
        rt1 = sb("rt1", [P, TT])
        rt2 = sb("rt2", [P, TT])
        sel = sb("sel", [P, TT, E])
        key = sb("key", [P, TT, E])
        hit = sb("hit", [P, TT, E])
        order = sb("order", [P, E])
        gate = sb("gate", [P, TT, E])
        prT = sb("prT", [P, P])
        cmp = sb("cmp", [P, P])
        cmp2 = sb("cmp2", [P, P])
        scan = sb("scan", [P, P])
        cnt = sb("cnt", [P, 2])
        cand = sb("cand", [P, 1], I32)
        fail = sb("fail", [P, 1], I32)
        need = sb("need", [P, 1])
        selT = sb("selT", [P, P])
        ones = sb("ones", [P, P])
        o_sq = arena[:, 0:G * NT * 2 * 2 * DH].rearrange("p (n d) -> p n d", d=2 * DH)
        o_tok = arena[:, 4096:4096 + TT * 2 * DH * H].rearrange("p (t g h d) -> p t g h d", t=TT, g=GB, h=2)
        o_flat = o_all[:, 1:1 + G, :, :, :].rearrange("p g t h d -> p (g t h) d")
        y = sb("y", [P, TT, D])

        bank = [ctx.enter_context(nc.psum_tensor(f"bank{i}", [P, BANK], F32)) for i in range(8)]
        ring_a, ring_b, pv = bank[0:3], bank[3:6], bank[6:8]

        s_x = sem("s_x")
        s_w = sem("s_w")
        s_const = sem("s_const")
        s_pool_const = sem("s_pool_const")
        s_proj = sem("s_proj")
        s_hi = sem("s_hi")
        s_rest = sem("s_rest")
        s_mid = sem("s_mid")
        s_lo = sem("s_lo")
        s_stored = sem("s_stored")
        s_vproj = sem("s_vproj")
        s_vcopy = sem("s_vcopy")
        s_vgrp = sem("s_vgrp")
        s_load = [sem(f"s_load{u}") for u in range(NBUF)]
        s_afill = sem("s_afill")
        s_afree = sem("s_afree")
        s_bfill = sem("s_bfill")
        s_bfree = sem("s_bfree")
        s_seen = sem("s_seen")
        s_mask = sem("s_mask")
        s_pfree = sem("s_pfree")
        s_ocopy = sem("s_ocopy")
        s_mchain = sem("s_mchain")
        s_shift = sem("s_shift")
        s_ochain = sem("s_ochain")
        s_lexp = sem("s_lexp")
        s_dchain = sem("s_dchain")
        s_ms = sem("s_ms")
        s_rms = sem("s_rms")
        s_onorm = sem("s_onorm")
        s_oct = sem("s_oct")
        s_octc = sem("s_octc")
        s_proj_o = sem("s_proj_o")
        s_x1sum = sem("s_x1sum")
        s_var = sem("s_var")
        s_std = sem("s_std")
        s_x1 = sem("s_x1")
        s_x1t = sem("s_x1t")
        s_x1tc = sem("s_x1tc")
        s_logit = sem("s_logit")
        s_lgsub = sem("s_lgsub")
        s_lgexp = sem("s_lgexp")
        s_prob = sem("s_prob")
        s_prt = sem("s_prt")
        s_count = sem("s_count")
        s_total = sem("s_total")
        s_tie = sem("s_tie")
        s_tiesum = sem("s_tiesum")
        s_selt = sem("s_selt")
        s_sel = sem("s_sel")
        s_gate = sem("s_gate")
        s_hid = sem("s_hid")
        s_gelu = sem("s_gelu")
        s_y = sem("s_y")
        s_yacc = sem("s_yacc")
        s_var2 = sem("s_var2")
        s_std2 = sem("s_std2")
        s_final = sem("s_final")
        s_out = sem("s_out")

        block = ctx.enter_context(nc.Block())

        @block.sync
        def _(sp):
            sp.dma_start(xT[:, 0:N], XT[:, 0:N]).then_inc(s_x, 16)
            sp.dma_start(wq[:, :], WqT).then_inc(s_x, 16)
            sp.dma_start(wk[:, :], WkT).then_inc(s_x, 16)
            sp.dma_start(xT[:, N:T], XT[:, N:T]).then_inc(s_x, 16)
            sp.dma_start(wv[:, :], WvT).then_inc(s_x, 16)
            small = [(lvec[:, m, :, :].rearrange("p h d -> p (h d)"),
                      v.rearrange("(a h) d -> a (h d)", a=1).partition_broadcast(P))
                     for m, v in enumerate((lq1, lk1, lq2, lk2))]
            small += [(rmscol[2 * DH * r:2 * DH * (r + 1), :], rms.rearrange("(n a) -> n a", a=1)) for r in range(P // (2 * DH))]
            small += [(ident[:, :], c_ident), (causalf[:, :], c_causal), (same[:, :], c_same), (before[:, :], c_before),
                      (wo[:, :, :], WoT.rearrange("(a p) n -> p a n", p=P)), (wg[:, :], Wg),
                      (w1[:, :, :], W1.rearrange("e p f -> p e f")),
                      (w2[:, :, :, :], W2.rearrange("e (a p) n -> p e a n", p=P)),
                      (x_tok[:, :, :], X.rearrange("b (t p) d -> p (b t) d", p=P))]
            for dst, src in small:
                sp.dma_start(dst, src).then_inc(s_w, 16)

            u = 0
            for b in range(B):
                for half in range(2):
                    for qk in range(2):
                        for t0 in (0, BANK):
                            sp.wait_ge(s_lo, u + 1)
                            for r in range(3):
                                f0 = (2 * b + half) * P
                                dst = parts_dram[qk, r, f0:f0 + P, t0:t0 + BANK]
                                sp.dma_start(dst, part_sb[u][:, r, :]).then_inc(s_stored, 16)
                            u += 1

            def load(g, buf):
                row, group, part = MAPS * N, MAPS * DH * N, G * MAPS * DH * N
                for r in range(3):
                    rows = slice(3 * r * DH, 3 * (r + 1) * DH)
                    q_src = bass.AP(parts_dram.tensor, g * group + r * part, [[0, 3], [row, DH], [1, row]])
                    k_src = bass.AP(parts_dram.tensor, g * group + 3 * part, [[part, 3], [row, DH], [1, row]])
                    sp.dma_start(q_op[buf][rows, :, :].rearrange("p c n -> p (c n)"), q_src).then_inc(s_load[buf], 16)
                    sp.dma_start(k_op[buf][rows, :, :].rearrange("p c n -> p (c n)"), k_src).then_inc(s_load[buf], 16)

            def shift(n_done, buf):
                sp.wait_ge(s_afree, n_done)
                for r in range(2):
                    sp.dma_start(q_op[buf][ROWS + r:ROWS + r + 1, :, :].rearrange("a c (t q) -> a (c t) q", t=NT),
                                 mT[r * MAPS * NT:(r + 1) * MAPS * NT, :]).then_inc(s_shift, 16)

            sp.wait_ge(s_const, 1)
            sp.wait_ge(s_stored, 48 * 16)
            load(0, 0)
            load(1, 1)
            shift(FIRST_A, 0)

            def body(it, u, loads=True):
                n3, n48 = it * (UNROLL * N_A), it * (UNROLL * N_SCORES)
                if loads:
                    sp.wait_ge(s_bfree, n48 + (u * N_SCORES + NRING))
                    load(it * UNROLL + (u + 2), (u + 2) % NBUF)
                shift(n3 + (FIRST_A + (u + 1) * N_A), (u + 1) % NBUF)

            loads_loops = (G - 2) // UNROLL
            with sp.Fori(0, loads_loops) as it:
                for u in range(UNROLL):
                    body(it, u)
            for n in range(loads_loops * UNROLL, G - 1):
                body(n // UNROLL, n % UNROLL, n + 2 < G)

            for b in range(B):
                sp.wait_ge(s_final, b + 1)
                sp.dma_start(out[b, :, :].rearrange("(t p) d -> p t d", p=P),
                             y[:, b * NT:(b + 1) * NT, :]).then_inc(s_out, 16)
            sp.wait_ge(s_out, 16 * B)

        @block.gpsimd
        def _(pool):
            nc.gpsimd.memset(v_grp[:, :, :, :, :], 0.0).then_inc(s_pool_const, 1)
            pool.wait_ge(s_pool_const, 1)
            nc.gpsimd.memset(v_grp[:, :, :, :, 2 * DH:2 * DH + 1], 1.0).then_inc(s_pool_const, 1)
            for e in range(E):
                nc.gpsimd.memset(order[:, e:e + 1], float(E - e)).then_inc(s_pool_const, 1)
            pool.wait_ge(s_pool_const, 2)
            pool.wait_ge(s_vcopy, TT)
            nc.gpsimd.tensor_copy(v_grp[:, 0, :, :, 0:2 * DH], v_all[:, 0, :, :, :]).then_inc(s_vgrp, 1)

            def body(it, u, last=False):
                n48 = it * (UNROLL * N_SCORES)
                for s in range(NT):
                    slot = (u * NT + s) % NSLOT
                    pool.wait_ge(s_bfree, n48 + (NRING + u * N_SCORES + SCORES_BEFORE[s + 1]))
                    pool.sem_inc(s_seen, 1)
                    nc.gpsimd.affine_select(out=probs[slot][:, :, 0:P], in_=probs[slot][:, :, 0:P], compare_op=ALU.is_ge,
                                            fill=0.0, base=0, pattern=[[0, MAPS], [1, P]],
                                            channel_multiplier=-1).then_inc(s_mask, 1)
                    if s == 3 and not last:
                        nxt = it * UNROLL + (u + 1)
                        nc.gpsimd.tensor_copy(v_grp[:, (u + 1) % NBUF, :, :, 0:2 * DH].rearrange("p h t d -> p (h t) d"),
                                              v_all[:, bass.ds(nxt, 1), :, :, :].rearrange("p a h t d -> p (a h t) d")).then_inc(s_vgrp, 1)

            with pool.Fori(0, LOOPS) as it:
                for u in range(UNROLL):
                    body(it, u)
            body(LOOPS, 0, last=True)

        @block.scalar
        def _(act):
            def mid(u):
                act.wait_ge(s_rest, u + 1)
                nc.scalar.activation(part_sb[u][:, 1, :], rest[:, u % 2, :], ACT.Copy).then_inc(s_mid, 1)

            for u in range(16):
                act.wait_ge(s_proj, u + 1)
                nc.scalar.activation(part_sb[u][:, 0, :], bank[u % 6][:, :], ACT.Copy).then_inc(s_hi, 1)
                if u >= 1:
                    mid(u - 1)
            mid(15)
            for t in range(TT):
                act.wait_ge(s_vproj, t + 1)
                b, i = t // NT, t % NT
                nc.scalar.activation(v_all[:, b * GB:(b + 1) * GB, :, i, :],
                                     bank[t % 6][:, 0:2 * DH * H].rearrange("p (g h d) -> p g h d", g=GB, h=2),
                                     ACT.Copy).then_inc(s_vcopy, 1)
            act.wait_ge(s_const, 5)
            nc.scalar.activation(lexp[:, :, :], lsum[:, :, :], ACT.Exp).then_inc(s_lexp, 1)
            act.sem_inc(s_bfree, NRING)
            act.sem_inc(s_ocopy, 2)
            act.wait_ge(s_stored, 48 * 16)

            def copy_out(it, u, last):
                act.wait_ge(s_pfree, it * (UNROLL * NT) + (NSLOT + (u + 1) * NT))
                act.wait_ge(s_afree, it * (UNROLL * N_A) + (FIRST_A + u * N_A + (2 if last else A_OUT_DONE)))
                for half in range(2):
                    nc.scalar.activation(oT[:, half * BANK:(half + 1) * BANK], pv[half][:, :], ACT.Copy).then_inc(s_ocopy, 1)

            def body(it, u, last):
                n48, n8 = it * (UNROLL * N_SCORES), it * (UNROLL * NT)
                for s in range(NT):
                    slot = (u * NT + s) % NSLOT
                    act.wait_ge(s_pfree, n8 + (u * NT + s + 1))
                    for k, (c, a, z) in enumerate(SCORE_UNITS[s]):
                        idx = u * N_SCORES + SCORES_BEFORE[s] + k
                        act.wait_ge(s_bfill, n48 + (idx + 1))
                        nc.scalar.activation(probs[slot][:, c, a - P * s:z - P * s], ring_b[idx % NRING][:, 0:z - a],
                                             ACT.Exp, scale=SCALE).then_inc(s_bfree, 1)
                copy_out(it, u, last)

            with act.Fori(0, LOOPS) as it:
                for u in range(UNROLL):
                    body(it, u, False)
            body(LOOPS, 0, True)

            act.wait_ge(s_ms, 1)
            nc.scalar.activation(ss[:, :], ss[:, :], ACT.Sqrt).then_inc(s_rms, 1)
            for t in range(TT):
                act.wait_ge(s_oct, t + 1)
                if t >= 2:
                    act.wait_ge(s_proj_o, t - 1)
                nc.scalar.activation(ocT[:, t % 2, :, :], bank[t % 2][:, 0:2 * D].rearrange("p (a n) -> p a n", a=2),
                                     ACT.Copy).then_inc(s_octc, 1)
            act.wait_ge(s_var, 1)
            nc.scalar.activation(rstd[:, :], rstd[:, :], ACT.Sqrt).then_inc(s_std, 1)
            for q in range(4):
                act.wait_ge(s_x1t, q + 1)
                nc.scalar.activation(xT[:, q * BANK:(q + 1) * BANK], bank[q][:, :], ACT.Copy).then_inc(s_x1tc, 1)
            act.wait_ge(s_lgsub, 1)
            nc.scalar.activation(key[:, :, :], pr[:, :, :], ACT.Exp).then_inc(s_lgexp, 1)
            for e in range(E):
                for f in range(2):
                    for q in range(4):
                        i = (e * 2 + f) * 4 + q
                        act.wait_ge(s_hid, i + 1)
                        if e >= HT_SLOTS:
                            act.wait_ge(s_y, 4 * (e - HT_SLOTS + 1))
                        nc.scalar.activation(hT[e % HT_SLOTS][:, f, q * BANK:(q + 1) * BANK], bank[5 + i % 3][:, :],
                                             ACT.Gelu).then_inc(s_gelu, 1)
            for b in range(B):
                act.wait_ge(s_var2, b + 1)
                nc.scalar.activation(rstd[:, b * NT:(b + 1) * NT], rstd[:, b * NT:(b + 1) * NT], ACT.Sqrt).then_inc(s_std2, 1)

        @block.vector
        def _(dve):
            nc.vector.memset(a_b[64:P, NBUF * nq:2 * NBUF * nq], 1.0).then_inc(s_const, 1)
            nc.vector.memset(oT[:, :], 1.0)
            nc.vector.memset(nlam[:, 0:1, :], 1.0)
            nc.vector.memset(m_parts[:, :, :], 0.0)
            nc.vector.memset(m_raw[:, :, :, :], -3.0e38).then_inc(s_const, 1)
            def low(u):
                dve.wait_ge(s_mid, u + 1)
                nc.vector.tensor_tensor(out=part_sb[u][:, 2, :], in0=rest[:, u % 2, :], in1=part_sb[u][:, 1, :],
                                        op=ALU.subtract).then_inc(s_lo, 1)

            for u in range(16):
                dve.wait_ge(s_hi, u + 1)
                if u >= 2:
                    dve.wait_ge(s_lo, u - 1)
                nc.vector.tensor_tensor(out=rest[:, u % 2, :], in0=bank[u % 6][:, :], in1=part_sb[u][:, 0, :],
                                        op=ALU.subtract).then_inc(s_rest, 1)
                if u >= 1:
                    low(u - 1)
            low(15)
            dve.wait_ge(s_w, 16 * N_SMALL)
            nc.vector.tensor_copy(identb[:, :], ident[:, :])
            nc.vector.tensor_copy(causalb[:, :], causalf[:, :]).then_inc(s_const, 1)
            nc.vector.tensor_tensor(out=lprod[:, :, :, :], in0=lvec[:, 0:4:2, :, :], in1=lvec[:, 1:4:2, :, :], op=ALU.mult).then_inc(s_const, 1)
            dve.wait_ge(s_const, 4)
            nc.vector.tensor_reduce(out=lsum[:, :, :], in_=lprod[:, :, :, :], axis=AX.X, op=ALU.add).then_inc(s_const, 1)
            dve.wait_ge(s_lexp, 1)
            for b in range(B):
                nc.vector.scalar_tensor_tensor(out=nlam[:, 1 + b * GB:1 + (b + 1) * GB, :].rearrange("p g h -> p (g h)"),
                                               in0=lexp[:, 1, :], scalar=-LAMBDA_INIT, in1=lexp[:, 0, :],
                                               op0=ALU.add, op1=ALU.subtract).then_inc(s_const, 1)
            dve.wait_ge(s_const, 7)

            def take_max(unit, idx):
                c, i, n, a, z = unit
                nc.vector.tensor_reduce(out=m_raw[:, c, i, n:n + 1], in_=ring_a[idx % NRING][:, 0:z - a],
                                        axis=AX.X, op=ALU.max).then_inc(s_afree, 1)

            def split_max(a_done, chain):
                dve.wait_ge(s_afree, a_done)
                nc.vector.tensor_reduce(out=m_neg[:, :], in_=m_raw[:, :, :, :].rearrange("p c t n -> p (c t) n"),
                                        axis=AX.X, op=ALU.max, negate=True).then_inc(s_mchain, 1)
                dve.wait_ge(s_mchain, chain + 1)
                nc.vector.tensor_copy(m_parts[:, 0, :], m_neg[:, :]).then_inc(s_mchain, 1)
                dve.wait_ge(s_mchain, chain + 2)
                nc.vector.tensor_tensor(out=m_parts[:, 1, :], in0=m_neg[:, :], in1=m_parts[:, 0, :],
                                        op=ALU.subtract).then_inc(s_mchain, 1)

            def copy_shift(idx, shifts):
                dve.wait_ge(s_shift, shifts)
                nc.vector.tensor_copy(mT[:, :], ring_a[idx % NRING][:, :].bitcast(BF16)[0:2 * MAPS * NT, 0:P]).then_inc(s_afree, 1)

            def normalise(it, u, half, idx, chain):
                o = ring_a[idx % NRING][:, :].rearrange("p (t c r) -> p t c r", t=4, c=MAPS)
                nc.vector.reciprocal(rinv[:, half, :, :], o[:, :, :, 2 * DH]).then_inc(s_ochain, 1)
                dve.wait_ge(s_ochain, chain + 1)
                slot = it * UNROLL + u
                lam = nlam[:, bass.ds(slot, 1), :].broadcast_to([P, 4, 2])
                nc.vector.tensor_tensor(out=rinv[:, half, :, 1:MAPS:2], in0=rinv[:, half, :, 1:MAPS:2], in1=lam,
                                        op=ALU.mult).then_inc(s_ochain, 1)
                dve.wait_ge(s_ochain, chain + 2)
                nc.vector.tensor_tensor(out=o_norm[:, half, :, :, :], in0=o[:, :, :, 0:2 * DH],
                                        in1=rinv[:, half, :, :].unsqueeze(3).broadcast_to([P, 4, MAPS, 2 * DH]),
                                        op=ALU.mult).then_inc(s_afree, 1)
                return chain + 2

            def combine(it, u, half, a_done):
                dve.wait_ge(s_afree, a_done)
                slot = it * UNROLL + u
                nc.vector.tensor_tensor(out=o_all[:, bass.ds(slot, 1), 4 * half:4 * half + 4, :, :].rearrange("p a t h d -> p (a t) h d"),
                                        in0=o_norm[:, half, :, 0:MAPS:2, :], in1=o_norm[:, half, :, 1:MAPS:2, :],
                                        op=ALU.add).then_inc(s_ochain, 1)

            idx = 0
            for step in range(NT):
                for unit in MAX_UNITS[step]:
                    dve.wait_ge(s_afill, idx + 1)
                    take_max(unit, idx)
                    idx += 1
            split_max(idx, 0)
            dve.wait_ge(s_afill, idx + 1)
            copy_shift(idx, 0)

            def body(it, u, last=False):
                na, nm, no = it * (UNROLL * N_A), it * (UNROLL * 3), it * (UNROLL * 6)
                a = FIRST_A + u * N_A
                chain_o = u * 6
                for s in range(NT):
                    for kind, what in a_items(s, last):
                        if kind == "max":
                            dve.wait_ge(s_afill, na + (a + 1))
                            take_max(what, a)
                        elif kind == "out":
                            dve.wait_ge(s_afill, na + (a + 1))
                            normalise(it, u, what, a, no + chain_o)
                            combine(it, u, what, na + (a + 1))
                            chain_o += 3
                        else:
                            dve.wait_ge(s_afill, na + (a + 1))
                            copy_shift(a, it * (UNROLL * 32) + 32 * (u + 1))
                        a += 1
                    if s == SPLIT_STEP and not last:
                        split_max(na + a, nm + 3 * (u + 1))

            with dve.Fori(0, LOOPS) as it:
                for u in range(UNROLL):
                    body(it, u)
            body(LOOPS, 0, last=True)
            a = FIRST_A + (G - 1) * N_A + 2
            for half in range(2):
                dve.wait_ge(s_afill, a + 1)
                normalise(G // UNROLL, G % UNROLL, half, a, 6 * G + 3 * half)
                combine(G // UNROLL, G % UNROLL, half, a + 1)
                a += 1

            chain = [0]

            def link(ins):
                chain[0] += 1
                ins.then_inc(s_dchain, 1)
                dve.wait_ge(s_dchain, chain[0])

            V = nc.vector
            dve.wait_ge(s_ochain, 6 * G + 6)
            link(V.tensor_tensor(out=o_sq, in0=o_flat, in1=o_flat, op=ALU.mult))
            link(V.tensor_reduce(out=ss[:, :], in_=o_sq, axis=AX.X, op=ALU.add))
            V.tensor_scalar(ss[:, :], ss[:, :], 1.0 / (2 * DH), EPS, ALU.mult, ALU.add).then_inc(s_ms, 1)
            link(V.tensor_scalar(wo[:, :, :], wo[:, :, :], rmscol[:, 0:1], 1.0 - LAMBDA_INIT, ALU.mult, ALU.mult))
            dve.wait_ge(s_rms, 1)
            link(V.reciprocal(ss[:, :], ss[:, :]))
            inv_rms = ss[:, :].rearrange("p (g t h) -> p g t h", g=G, t=NT)
            for b in range(B):
                for h in range(2):
                    gs = slice(b * GB, (b + 1) * GB)
                    last = V.tensor_tensor(out=o_tok[:, b * NT:(b + 1) * NT, :, h, :].rearrange("p t g d -> p g t d"),
                                           in0=o_all[:, 1 + b * GB:1 + (b + 1) * GB, :, h, :],
                                           in1=inv_rms[:, gs, :, h].unsqueeze(3).broadcast_to([P, GB, NT, 2 * DH]), op=ALU.mult)
            last.then_inc(s_onorm, 1)
            for t in range(TT):
                dve.wait_ge(s_proj_o, t + 1)
                V.tensor_tensor(out=x_tok[:, t, :], in0=bank[2 + t % 2][:, 0:D], in1=x_tok[:, t, :], op=ALU.add).then_inc(s_x1sum, 1)
                dve.wait_ge(s_x1sum, t + 1)
                link(V.bn_stats(stats[:, t, :], x_tok[:, t, :]))
                link(V.bn_aggr(mv[:, t, :], stats[:, t, :]))
            V.tensor_scalar(rstd[:, :], mv[:, :, 1], EPS, None, ALU.add).then_inc(s_var, 1)
            dve.wait_ge(s_std, 1)
            link(V.reciprocal(rstd[:, :], rstd[:, :]))
            for t in range(TT):
                last = V.tensor_scalar(x_tok[:, t, :], x_tok[:, t, :], mv[:, t, 0:1], rstd[:, t:t + 1], ALU.subtract, ALU.mult)
                if t % 4 == 3:
                    last.then_inc(s_x1, 1)

            def wide(x):
                return x.unsqueeze(2).broadcast_to([P, TT, E])

            dve.wait_ge(s_logit, 1)
            link(V.tensor_copy(lg[:, :, :], bank[4][:, 0:TT * E].rearrange("p (t e) -> p t e", e=E)))
            link(V.tensor_reduce(out=rt1[:, :], in_=lg[:, :, :], axis=AX.X, op=ALU.max))
            V.tensor_tensor(out=pr[:, :, :], in0=lg[:, :, :], in1=wide(rt1[:, :]), op=ALU.subtract).then_inc(s_lgsub, 1)
            dve.wait_ge(s_lgexp, 1)
            link(V.tensor_reduce(out=rt2[:, :], in_=key[:, :, :], axis=AX.X, op=ALU.add))
            link(V.reciprocal(rt2[:, :], rt2[:, :]))
            V.tensor_tensor(out=pr[:, :, :], in0=key[:, :, :], in1=wide(rt2[:, :]), op=ALU.mult).then_inc(s_prob, 1)
            dve.wait_ge(s_prt, 1)
            V.memset(cand[:, :], 1 << (N_BITS - 1))
            V.memset(ones[:, :], 1.0)
            link(V.tensor_copy(prT[:, :], bank[0][:, 0:P]))
            threshold = cand[:, 0:1].bitcast(F32)
            for k in range(N_BITS):
                bit, following = 1 << (N_BITS - 1 - k), (1 << (N_BITS - 1 - k)) >> 1
                V.tensor_scalar(cmp[:, :], prT[:, :], threshold, None, ALU.is_ge, ALU.add, accum_out=cnt[:, 0:1]).then_inc(s_count, 1)
                dve.wait_ge(s_total, k + 1)
                link(V.tensor_scalar(fail[:, :], bank[1][:, 0:1], float(CAP), float(bit), ALU.is_lt, ALU.mult))
                link(V.scalar_tensor_tensor(out=cand[:, :], in0=cand[:, :], scalar=following, in1=fail[:, :],
                                            op0=ALU.bitwise_xor, op1=ALU.bitwise_xor))
            link(V.tensor_scalar(cmp[:, :], prT[:, :], threshold, None, ALU.is_gt, ALU.add, accum_out=cnt[:, 0:1]))
            V.tensor_scalar(cmp2[:, :], prT[:, :], threshold, None, ALU.is_equal, ALU.add, accum_out=cnt[:, 1:2]).then_inc(s_tie, 1)
            dve.wait_ge(s_tie, 1)
            link(V.tensor_tensor_scan(out=scan[:, :], data0=ones[:, :], data1=cmp2[:, :], initial=0.0, op0=ALU.mult, op1=ALU.add))
            dve.wait_ge(s_tiesum, 1)
            link(V.tensor_scalar(need[:, :], bank[1][:, 8:9], -1.0, float(CAP), ALU.mult, ALU.add))
            link(V.tensor_tensor(out=need[:, :], in0=need[:, :], in1=bank[1][:, 16:17], op=ALU.subtract))
            link(V.scalar_tensor_tensor(out=cmp2[:, :], in0=scan[:, :], scalar=need[:, 0:1], in1=cmp2[:, :],
                                        op0=ALU.is_le, op1=ALU.mult))
            V.tensor_tensor(out=selT[:, :], in0=cmp[:, :], in1=cmp2[:, :], op=ALU.add).then_inc(s_selt, 1)
            dve.wait_ge(s_sel, 1)
            link(V.tensor_copy(sel[:, :, :], bank[2][:, 0:P].rearrange("p (t e) -> p t e", e=E)))
            link(V.tensor_reduce(out=rt1[:, :], in_=sel[:, :, :], axis=AX.X, op=ALU.max))
            link(V.tensor_scalar(rt1[:, :], rt1[:, :], -1.0, 1.0, ALU.mult, ALU.add))
            link(V.tensor_tensor(out=sel[:, :, :], in0=sel[:, :, :], in1=wide(rt1[:, :]), op=ALU.add))
            link(V.tensor_tensor(out=key[:, :, :], in0=pr[:, :, :], in1=sel[:, :, :], op=ALU.mult))
            link(V.scalar_tensor_tensor(out=key[:, :, :], in0=sel[:, :, :], scalar=-1.0, in1=key[:, :, :],
                                        op0=ALU.add, op1=ALU.add))
            link(V.tensor_reduce(out=rt2[:, :], in_=key[:, :, :], axis=AX.X, op=ALU.max))
            link(V.tensor_tensor(out=hit[:, :, :], in0=key[:, :, :], in1=wide(rt2[:, :]), op=ALU.is_equal))
            dve.wait_ge(s_pool_const, 2 + E)
            link(V.tensor_tensor(out=hit[:, :, :], in0=hit[:, :, :], in1=order[:, :].unsqueeze(1).broadcast_to([P, TT, E]),
                                 op=ALU.mult))
            link(V.tensor_reduce(out=rt1[:, :], in_=hit[:, :, :], axis=AX.X, op=ALU.max))
            link(V.tensor_tensor(out=hit[:, :, :], in0=hit[:, :, :], in1=wide(rt1[:, :]), op=ALU.is_equal))
            V.tensor_tensor(out=gate[:, :, :], in0=hit[:, :, :], in1=pr[:, :, :], op=ALU.mult).then_inc(s_gate, 1)
            dve.wait_ge(s_gate, 1)
            for e in range(E):
                for q in range(4):
                    dve.wait_ge(s_y, 4 * e + q + 1)
                    if e >= 1:
                        dve.wait_ge(s_yacc, 4 * (e - 1) + q + 1)
                    for t in range(4 * q, 4 * q + 4):
                        last = V.scalar_tensor_tensor(out=y[:, t, :], in0=bank[q][:, (t % 4) * D:(t % 4 + 1) * D],
                                                      scalar=gate[:, t, e:e + 1], in1=(y if e else x_tok)[:, t, :],
                                                      op0=ALU.mult, op1=ALU.add)
                    last.then_inc(s_yacc, 1)
            dve.wait_ge(s_yacc, 4 * E)
            for b in range(B):
                tiles = range(b * NT, (b + 1) * NT)
                for t in tiles:
                    last = V.bn_stats(stats[:, t, :], y[:, t, :])
                link(last)
                for t in tiles:
                    last = V.bn_aggr(mv[:, t, :], stats[:, t, :])
                link(last)
                V.tensor_scalar(rstd[:, b * NT:(b + 1) * NT], mv[:, b * NT:(b + 1) * NT, 1], EPS, None, ALU.add).then_inc(s_var2, 1)
            for b in range(B):
                dve.wait_ge(s_std2, b + 1)
                link(V.reciprocal(rstd[:, b * NT:(b + 1) * NT], rstd[:, b * NT:(b + 1) * NT]))
                for t in range(b * NT, (b + 1) * NT):
                    last = V.tensor_scalar(y[:, t, :], y[:, t, :], mv[:, t, 0:1], rstd[:, t:t + 1], ALU.subtract, ALU.mult)
                last.then_inc(s_final, 1)

        @block.tensor
        def _(pe):
            pe.wait_ge(s_x, 16 * 5)
            u = 0
            for b in range(B):
                for half in range(2):
                    for w in (wq, wk):
                        for t0 in (0, BANK):
                            if u >= 6:
                                pe.wait_ge(s_rest, u - 5)
                            nc.tensor.matmul(bank[u % 6][:, :], w[:, half * P:(half + 1) * P],
                                             xT[:, b * N + t0:b * N + t0 + BANK], start=True, stop=True).then_inc(s_proj, 1)
                            u += 1
            for t in range(TT):
                if t < 6:
                    pe.wait_ge(s_rest, 16)
                else:
                    pe.wait_ge(s_vcopy, t - 5)
                nc.tensor.matmul(bank[t % 6][:, 0:2 * DH * H], xT[:, t * P:(t + 1) * P], wv[:, :],
                                 start=True, stop=True).then_inc(s_vproj, 1)

            def max_unit(buf, unit, idx, free):
                c, i, n, a, z = unit
                if free is not None:
                    pe.wait_ge(s_afree, free)
                dst = ring_a[idx % NRING]
                masked = z == P * (i + 1)
                last = nc.tensor.matmul(dst[:, 0:z - a], q_op[buf][0:ROWS, c, i * P:(i + 1) * P],
                                        k_op[buf][0:ROWS, c, a:z], start=True, stop=not masked)
                if masked:
                    last = nc.tensor.matmul(dst[:, z - a - P:z - a], identb[:, :], causalb[:, :], start=False, stop=True)
                last.then_inc(s_afill, 1)

            def shift_unit(idx, chain, free):
                pe.wait_ge(s_mchain, chain)
                pe.wait_ge(s_afree, free)
                nc.tensor.transpose(ring_a[idx % NRING][:, :].bitcast(BF16)[:, 0:P],
                                    m_parts[:, :, :].rearrange("p r n -> p (r n)"), identb[:, :]).then_inc(s_afill, 1)

            def out_unit(half, idx, free):
                pe.wait_ge(s_afree, free)
                for t in range(4):
                    last = nc.tensor.transpose(ring_a[idx % NRING][:, t * P:(t + 1) * P],
                                               oT[:, half * BANK + t * P:half * BANK + (t + 1) * P], ident[:, :])
                last.then_inc(s_afill, 1)

            pe.wait_ge(s_const, 7)
            pe.wait_ge(s_vcopy, TT)
            pe.wait_ge(s_load[0], LOAD_INC)
            idx = 0
            for step in range(NT):
                for unit in MAX_UNITS[step]:
                    max_unit(0, unit, idx, idx - 2 if idx >= NRING else None)
                    idx += 1
            shift_unit(idx, 3, idx - 2)

            def pv_step(it, u, s):
                n8 = it * (UNROLL * NT)
                t = u * NT + s
                if s == 0:
                    pe.wait_ge(s_vgrp, it * UNROLL + (u + 1))
                    pe.wait_ge(s_ocopy, it * (UNROLL * 2) + 2 * (u + 1))
                pe.wait_ge(s_mask, n8 + (t + 1))
                for a, z in spans(P * s, N):
                    half = a // BANK
                    for c in range(MAPS):
                        last = nc.tensor.matmul(pv[half][32 * c:32 * c + 32, a - half * BANK:z - half * BANK],
                                                v_grp[:, u % NBUF, c // 2, s, :],
                                                probs[t % NSLOT][:, c, a - P * s:z - P * s],
                                                start=s == 0, stop=s == (3 if half == 0 else 7))
                last.then_inc(s_pfree, 1)

            def body(it, u, last=False):
                na, nb = it * (UNROLL * N_A), it * (UNROLL * N_SCORES)
                a = FIRST_A + u * N_A
                pe.wait_ge(s_shift, it * (UNROLL * 32) + 32 * (u + 1))
                if not last:
                    load_turn = (u + 1) // NBUF
                    pe.wait_ge(s_load[(u + 1) % NBUF], it * LOAD_INC + (load_turn + 1) * LOAD_INC)
                for s in range(NT):
                    work = interleave([("score", x) for x in SCORE_UNITS[s]], a_items(s, last))
                    k = 0
                    for kind, what in work:
                        if kind == "score":
                            c, lo, hi = what
                            b_idx = u * N_SCORES + SCORES_BEFORE[s] + k
                            k += 1
                            pe.wait_ge(s_bfree, nb + (b_idx + 1))
                            nc.tensor.matmul(ring_b[b_idx % NRING][:, 0:hi - lo], k_op[u % NBUF][0:SROWS, c, s * P:(s + 1) * P],
                                             q_op[u % NBUF][0:SROWS, c, lo:hi], start=True, stop=True).then_inc(s_bfill, 1)
                            continue
                        if kind == "max":
                            max_unit((u + 1) % NBUF, what, a, na + (a - 2))
                        elif kind == "out":
                            out_unit(what, a, na + (a - 2))
                        else:
                            shift_unit(a, it * (UNROLL * 3) + 3 * (u + 2), na + (a - 2))
                        a += 1
                    if s >= 1:
                        pv_step(it, u, s - 1)
                pv_step(it, u, NT - 1)

            pe.sem_inc(s_pfree, NSLOT)
            with pe.Fori(0, LOOPS) as it:
                for u in range(UNROLL):
                    body(it, u)
            body(LOOPS, 0, last=True)
            a = FIRST_A + (G - 1) * N_A + 2
            pe.wait_ge(s_ocopy, 2 * (G + 1))
            for half in range(2):
                out_unit(half, a, a - 2)
                a += 1

            def project(t):
                pe.wait_ge(s_octc, t + 1)
                if t >= 2:
                    pe.wait_ge(s_x1sum, t - 1)
                for a in range(2):
                    last = nc.tensor.matmul(bank[2 + t % 2][:, 0:D], ocT[:, t % 2, a, :], wo[:, a, :], start=a == 0, stop=a == 1)
                last.then_inc(s_proj_o, 1)

            pe.wait_ge(s_onorm, 1)
            for t in range(TT):
                if t >= 2:
                    pe.wait_ge(s_octc, t - 1)
                for a in range(2):
                    last = nc.tensor.transpose(bank[t % 2][:, a * P:(a + 1) * P],
                                               o_tok[:, t, 4 * a:4 * a + 4, :, :].rearrange("p g h d -> p (g h d)"), ident[:, :])
                last.then_inc(s_oct, 1)
                if t >= 1:
                    project(t - 1)
            project(TT - 1)
            for q in range(4):
                pe.wait_ge(s_x1, q + 1)
                for t in range(4):
                    last = nc.tensor.transpose(bank[q][:, t * P:(t + 1) * P], x_tok[:, 4 * q + t, :], ident[:, :])
                last.then_inc(s_x1t, 1)
            for t in range(TT):
                if t % 4 == 0:
                    pe.wait_ge(s_x1tc, t // 4 + 1)
                last = nc.tensor.matmul(bank[4][:, t * E:(t + 1) * E], xT[:, t * P:(t + 1) * P], wg[:, :], start=True, stop=True)
            last.then_inc(s_logit, 1)

            def hidden(i):
                e, f, q = i // 8, i // 4 % 2, i % 4
                if i >= 3:
                    pe.wait_ge(s_gelu, i - 2)
                nc.tensor.matmul(bank[5 + i % 3][:, :], w1[:, e, f * P:(f + 1) * P], xT[:, q * BANK:(q + 1) * BANK],
                                 start=True, stop=True).then_inc(s_hid, 1)

            def expert_out(e):
                pe.wait_ge(s_gelu, 8 * (e + 1))
                for q in range(4):
                    if e >= 1:
                        pe.wait_ge(s_yacc, 4 * (e - 1) + q + 1)
                    for t in range(4):
                        for f in range(2):
                            last = nc.tensor.matmul(bank[q][:, t * D:(t + 1) * D],
                                                    hT[e % HT_SLOTS][:, f, (4 * q + t) * P:(4 * q + t + 1) * P],
                                                    w2[:, e, f, :], start=f == 0, stop=f == 1)
                    last.then_inc(s_y, 1)

            for i in range(8 * HT_SLOTS):
                hidden(i)
                if i == 4:
                    pe.wait_ge(s_prob, 1)
                    nc.tensor.transpose(bank[0][:, 0:P], pr[:, :, :].rearrange("p t e -> p (t e)"), ident[:, :]).then_inc(s_prt, 1)
                if 5 <= i < 5 + N_BITS:
                    pe.wait_ge(s_count, i - 4)
                    nc.tensor.matmul(bank[1][:, 0:1], same[:, :], cnt[:, 0:1], start=True, stop=True).then_inc(s_total, 1)
                if i == 5 + N_BITS + 1:
                    pe.wait_ge(s_tie, 1)
                    nc.tensor.matmul(bank[1][:, 8:9], same[:, :], cnt[:, 0:1], start=True, stop=True)
                    nc.tensor.matmul(bank[1][:, 16:17], before[:, :], cnt[:, 1:2], start=True, stop=True).then_inc(s_tiesum, 1)
                if i == 5 + N_BITS + 3:
                    pe.wait_ge(s_selt, 1)
                    nc.tensor.transpose(bank[2][:, 0:P], selT[:, :], ident[:, :]).then_inc(s_sel, 1)
            pe.wait_ge(s_gate, 1)
            for e in range(E):
                expert_out(e)
                if HT_SLOTS + e < E:
                    for i in range(8 * (HT_SLOTS + e), 8 * (HT_SLOTS + e + 1)):
                        hidden(i)


_INS = ["X", "XT", "WqT", "WkT", "WvT", "WoT", "lq1", "lk1", "lq2", "lk2", "rms", "Wg", "W1", "W2",
        "c_ident", "c_causal", "c_same", "c_before"]


def kernel(**inputs):
    import numpy as np
    import concourse.bacc as bacc
    from concourse.bass_utils import run_bass_kernel_spmd

    x = np.asarray(inputs["L0_attn_X"])
    arrays = {"X": x, "XT": x.reshape(T, D).T}
    for n in ("Wq", "Wk", "Wv", "Wo"):
        arrays[n + "T"] = np.asarray(inputs[f"L0_attn_{n}"]).T
    for n in ("WqT", "WkT"):
        arrays[n] = arrays[n].reshape(D, GB, MAPS, DH).transpose(0, 1, 3, 2).reshape(D, 2 * DH * H)
    for n in ("lq1", "lk1", "lq2", "lk2"):
        arrays[n] = inputs[f"L0_attn_{n}"]
    arrays["rms"] = inputs["L0_attn_rms_scale"]
    for n in ("Wg", "W1", "W2"):
        arrays[n] = inputs[f"L0_ffn_{n}"]
    p = np.arange(P)
    same_expert = (p[:, None] - p[None, :]) % E == 0
    arrays["c_ident"] = np.eye(P, dtype=np.float32)
    arrays["c_causal"] = np.where(p[None, :] > p[:, None], np.float32(-1e30), np.float32(0))
    arrays["c_same"] = same_expert.astype(np.float32)
    arrays["c_before"] = (same_expert & (p[:, None] < p[None, :])).astype(np.float32)

    nc = bacc.Bacc("TRN2", target_bir_lowering=False, num_devices=1)
    ins = {f"in_{n}": np.ascontiguousarray(arrays[n]) for n in _INS}
    args = [nc.dram_tensor(n, a.shape, mybir.dt.from_np(a.dtype), kind="ExternalInput").ap() for n, a in ins.items()]
    args.append(nc.dram_tensor("out", (B, N, D), F32, kind="ExternalOutput").ap())
    build(nc, *args)
    return run_bass_kernel_spmd(nc, [ins], core_ids=[0]).results[0]["out"]
```

```python
from contextlib import ExitStack

import concourse.bass as bass
from concourse import mybir

ALU = mybir.AluOpType
ACT = mybir.ActivationFunctionType
AX = mybir.AxisListType
F32 = mybir.dt.float32
BF16 = mybir.dt.bfloat16
I32 = mybir.dt.int32

B, N, D = 2, 1024, 128
H, DH = 16, 8
E, F = 8, 256
T = B * N
CAP = T // E
LAMBDA_INIT, EPS = 0.8, 1e-5
SCALE = float(DH) ** -0.5

P = 128
BANK = 512
NT = N // P
TT = T // P
MAPS = 4
GB = 2 * H // MAPS
G = B * GB
ROWS = 9 * DH
SROWS = ROWS + 2
NBUF = 3
NRING = 3
NSLOT = 3
UNROLL = NBUF
LOOPS = (G - 3) // UNROLL

MAX_FIRST, MAX_EARLY = [7, 6, 5, 4], [3, 2, 1, 0]
INVERT_AT = 44
SHIFT_LAG = 6
COPY_STEP = 0
LATENCY, MASK_TIME, PACE, FAR = 400, 2500, 0.9, 1 << 30
LAG = 2
O_STEP = 4


def spans(lo, hi):
    out = []
    while lo < hi:
        end = min(hi, (lo // BANK + 1) * BANK)
        out.append((lo, end))
        lo = end
    return out


SCORE_UNITS = [[(c, a, z) for c in range(MAPS) for a, z in spans(P * j, N)] for j in range(NT)]
LOAD_INC = 7 * 16
N_SMALL = 4 + P // (2 * DH) + 9
N_BITS = 30


def max_units(tiles):
    return [("max", (c, i, n, a, z)) for i in tiles for c in range(MAPS) for n, (a, z) in enumerate(spans(0, P * (i + 1)))]


def a_items(n):
    items = max_units(MAX_FIRST) if n + 1 < G else []
    done = len(items)
    if n + 2 < G:
        items += [("early", x) for _, x in max_units(MAX_EARLY)]
    if n + 1 < G:
        items.insert(min(done + SHIFT_LAG, len(items)), ("shift", None))
    return items


def b_items(step):
    items = [("score", (step, c, a, z)) for c in range(MAPS) for a, z in spans(P * step, N)]
    if step == O_STEP:
        items += [("out", 0), ("out", 1)]
    return items


def a_before(n):
    return FIRST_A + sum(len(a_items(m)) for m in range(n))


def pe_order(n):
    scores = [x for s in range(NT) for x in b_items(s)]
    maxima = a_items(n)
    first = -LAG if n else 0
    products = [(t, span) for t in range(first, NT - LAG) for span in spans(P * (t % NT), N)]
    a_done, b_done, masked = [0] * NRING, [0] * NRING, dict.fromkeys(range(-LAG, 0), MASK_TIME)

    def pe_cost(kind, what):
        if kind in ("shift", "out"):
            return 8 * P
        a, z = what[-2:]
        return z - a + (P if kind in ("max", "early") and z % P == 0 and z == P * (what[1] + 1) else 0)

    def reader_cost(kind, what, rate, fixed):
        return rate * (4 * P if kind in ("shift", "out") else what[-1] - what[-2]) + fixed

    work = sum(pe_cost(*x) for x in scores + maxima) + sum(4.4 * (z - a) for _, (a, z) in products)
    pace = PACE * work / max(1, sum(reader_cost(*x, 2.5, 150) for x in maxima))
    order, now, due = [], 0, 0
    drained = None if n else 0
    copied = n == 0
    while scores or maxima or products:
        t_a = max(now, a_done[-NRING] + LATENCY) if maxima else FAR
        t_b = max(now, b_done[-NRING] + LATENCY) if scores else FAR
        if not copied and drained is not None and COPY_STEP in masked:
            b_done[-1] = max(b_done[-1], drained + LATENCY) + 4 * BANK
            masked[0] = max(masked[0], b_done[-1] + LATENCY)
            copied = True
        t_p = max(now, masked.get(products[0][0], FAR)) if products else FAR
        if products and products[0][0] == 0 and not copied:
            t_p = FAR
        if scores and scores[0][0] == "score" and products and products[0][0] <= scores[0][1][0] - NSLOT:
            t_b = FAR
        if t_a <= now and due <= now:
            pick = "a"
        elif t_b <= now:
            pick = "b"
        elif t_p <= now:
            pick = "products"
        else:
            now = min(t_a, t_b, t_p)
            pick = "a" if t_a == now else "b" if t_b == now else "products"
        if pick == "a":
            x = maxima.pop(0)
            now += pe_cost(*x)
            took = reader_cost(*x, 2.5, 150)
            a_done.append(max(now + LATENCY, a_done[-1]) + took)
            due += took * pace
            order.append(("a", *x))
        elif pick == "b":
            x = scores.pop(0)
            now += pe_cost(*x)
            b_done.append(max(now + LATENCY, b_done[-1]) + reader_cost(*x, 2, 120))
            order.append(("b", *x))
            if x[0] == "score" and (not scores or scores[0][0] == "out" or scores[0][1][0] > x[1][0]):
                masked[x[1][0]] = b_done[-1] + MASK_TIME
        else:
            t, (a, z) = products.pop(0)
            now += 4.4 * (z - a)
            order.append(("products", t, (a, z)))
            drained = now if t == -1 else drained
    return order


B_BEFORE = [sum(len(b_items(t)) for t in range(s)) for s in range(NT + 1)]
N_B = B_BEFORE[-1]
N_A = len(a_items(0))
ALL_MAX, EARLY_MAX = max_units(MAX_FIRST + MAX_EARLY), max_units(MAX_EARLY)
FIRST_A = len(ALL_MAX) + 1 + len(EARLY_MAX)
OUT_AT = B_BEFORE[O_STEP + 1]
assert UNROLL * N_A % NRING == 0 and UNROLL * N_B % NRING == 0 and UNROLL * NT % NSLOT == 0


def build(nc, X, XT, WqT, WkT, WvT, WoT, lq1, lk1, lq2, lk2, rms, Wg, W1, W2, c_ident, c_causal, c_same, c_before, out):
    parts_dram = nc.dram_tensor("parts", (2, 3, G * MAPS * DH, N), BF16).ap()

    ctx = ExitStack()
    with ctx:
        def sb(name, shape, dt=F32):
            return ctx.enter_context(nc.sbuf_tensor(name, shape, dt))

        def sem(name):
            return ctx.enter_context(nc.semaphore(name))

        x_tok = sb("x_tok", [P, TT, D])
        xT = sb("xT", [P, T])
        wq, wk, wv = (sb(n, [P, 2 * DH * H]) for n in ("wq", "wk", "wv"))
        wo = sb("wo", [P, 2, D])
        wg = sb("wg", [P, E])
        w1 = sb("w1", [P, E, F])
        w2 = sb("w2", [P, E, 2, D])
        ident = sb("ident", [P, P])
        identb = sb("identb", [P, P], BF16)
        causalf = sb("causalf", [P, P])
        causalb = sb("causalb", [P, P], BF16)
        same = sb("same", [P, P])
        before = sb("before", [P, P])
        lvec = sb("lvec", [P, 4, H, DH])
        lprod = sb("lprod", [P, 2, H, DH])
        lsum = sb("lsum", [P, 2, H])
        lexp = sb("lexp", [P, 2, H])
        nlam = sb("nlam", [P, G + 1, 2])
        rmscol = sb("rmscol", [P, 1])
        arena = sb("arena", [P, 6 * 4096])
        HT_SLOTS = 6
        a_b = arena[:, :].bitcast(BF16)
        nq = MAPS * N
        q_op = [a_b[:, u * nq:(u + 1) * nq].rearrange("p (c n) -> p c n", c=MAPS) for u in range(NBUF)]
        k_op = [a_b[:, (NBUF + u) * nq:(NBUF + u + 1) * nq].rearrange("p (c n) -> p c n", c=MAPS) for u in range(NBUF)]
        p_at = NBUF * nq
        probs = [arena[:, p_at + s * nq:p_at + (s + 1) * nq].rearrange("p (c n) -> p c n", c=MAPS) for s in range(NSLOT)]
        pa = 2 * p_at
        part_sb = [a_b[:, pa + u * 3 * BANK:pa + (u + 1) * 3 * BANK].rearrange("p (r n) -> p r n", r=3) for u in range(16)]
        hT = [arena[:, s * 4096:(s + 1) * 4096].rearrange("p (f n) -> p f n", f=2) for s in range(HT_SLOTS)]
        rest = sb("rest", [P, 2, BANK])
        v_all = sb("v_all", [P, G, 2, NT, 2 * DH])
        v_grp = sb("v_grp", [P, NBUF, 2, NT, 32])
        oT = sb("oT", [P, N])
        o_all = sb("o_all", [P, G + 1, NT, 2, 2 * DH])
        o_tr = sb("o_tr", [P, NT, MAPS, 32])
        rinv = sb("rinv", [P, NT, MAPS])
        o_norm = sb("o_norm", [P, NT, MAPS, 2 * DH])
        o_two = sb("o_two", [P, NT, 2, 2 * DH])
        m_raw = sb("m_raw", [P, MAPS, NT, 2])
        m_neg = sb("m_neg", [P, MAPS * NT])
        m_parts = sb("m_parts", [P, 4, MAPS * NT], BF16)
        mT = sb("mT", [2 * MAPS * NT, P], BF16)
        ss = sb("ss", [P, G * NT * 2])
        stats = sb("stats", [P, TT, 6])
        mv = sb("mv", [P, TT, 2])
        rstd = sb("rstd", [P, TT])
        ocT = sb("ocT", [P, 2, 2, D])
        lg = sb("lg", [P, TT, E])
        pr = sb("pr", [P, TT, E])
        rt1 = sb("rt1", [P, TT])
        rt2 = sb("rt2", [P, TT])
        sel = sb("sel", [P, TT, E])
        key = sb("key", [P, TT, E])
        hit = sb("hit", [P, TT, E])
        order = sb("order", [P, E])
        gate = sb("gate", [P, TT, E])
        prT = sb("prT", [P, P])
        cmp = sb("cmp", [P, P])
        cmp2 = sb("cmp2", [P, P])
        scan = sb("scan", [P, P])
        cnt = sb("cnt", [P, 2])
        cand = sb("cand", [P, 1], I32)
        fail = sb("fail", [P, 1], I32)
        need = sb("need", [P, 1])
        selT = sb("selT", [P, P])
        ones = sb("ones", [P, P])
        o_sq = arena[:, 0:G * NT * 2 * 2 * DH].rearrange("p (n d) -> p n d", d=2 * DH)
        o_tok = arena[:, 4096:4096 + TT * 2 * DH * H].rearrange("p (t g h d) -> p t g h d", t=TT, g=GB, h=2)
        o_flat = o_all[:, 1:1 + G, :, :, :].rearrange("p g t h d -> p (g t h) d")
        y = o_all[:, 0:8, :, :, :].rearrange("p g t h d -> p (g t h d)").rearrange("p (t d) -> p t d", d=D)

        bank = [ctx.enter_context(nc.psum_tensor(f"bank{i}", [P, BANK], F32)) for i in range(8)]
        ring_a, ring_b, pv = bank[0:3], bank[3:6], bank[6:8]

        s_x = sem("s_x")
        s_w = sem("s_w")
        s_const = sem("s_const")
        s_pool_const = sem("s_pool_const")
        s_proj = sem("s_proj")
        s_hi = sem("s_hi")
        s_rest = sem("s_rest")
        s_mid = sem("s_mid")
        s_lo = sem("s_lo")
        s_stored = sem("s_stored")
        s_vproj = sem("s_vproj")
        s_vcopy = sem("s_vcopy")
        s_vgrp = sem("s_vgrp")
        s_load = [sem(f"s_load{u}") for u in range(NBUF)]
        s_afill = sem("s_afill")
        s_afree = sem("s_afree")
        s_bfill = sem("s_bfill")
        s_bfree = sem("s_bfree")
        s_seen = sem("s_seen")
        s_mask = sem("s_mask")
        s_pfree = sem("s_pfree")
        s_ocopy = sem("s_ocopy")
        s_mchain = sem("s_mchain")
        s_shift = sem("s_shift")
        s_ouse = sem("s_ouse")
        s_rinv = sem("s_rinv")
        s_ochain = sem("s_ochain")
        s_lexp = sem("s_lexp")
        s_dchain = sem("s_dchain")
        s_ms = sem("s_ms")
        s_rms = sem("s_rms")
        s_onorm = sem("s_onorm")
        s_oct = sem("s_oct")
        s_octc = sem("s_octc")
        s_proj_o = sem("s_proj_o")
        s_x1sum = sem("s_x1sum")
        s_var = sem("s_var")
        s_std = sem("s_std")
        s_x1 = sem("s_x1")
        s_x1t = sem("s_x1t")
        s_x1tc = sem("s_x1tc")
        s_logit = sem("s_logit")
        s_lgsub = sem("s_lgsub")
        s_lgexp = sem("s_lgexp")
        s_prob = sem("s_prob")
        s_prt = sem("s_prt")
        s_count = sem("s_count")
        s_total = sem("s_total")
        s_tie = sem("s_tie")
        s_tiesum = sem("s_tiesum")
        s_selt = sem("s_selt")
        s_sel = sem("s_sel")
        s_gate = sem("s_gate")
        s_hid = sem("s_hid")
        s_gelu = sem("s_gelu")
        s_y = sem("s_y")
        s_yacc = sem("s_yacc")
        s_var2 = sem("s_var2")
        s_std2 = sem("s_std2")
        s_final = sem("s_final")
        s_out = sem("s_out")

        block = ctx.enter_context(nc.Block())

        @block.sync
        def _(sp):
            sp.dma_start(xT[:, 0:N], XT[:, 0:N]).then_inc(s_x, 16)
            sp.dma_start(wq[:, :], WqT).then_inc(s_x, 16)
            sp.dma_start(wk[:, :], WkT).then_inc(s_x, 16)
            sp.dma_start(xT[:, N:T], XT[:, N:T]).then_inc(s_x, 16)
            sp.dma_start(wv[:, :], WvT).then_inc(s_x, 16)
            small = [(lvec[:, m, :, :].rearrange("p h d -> p (h d)"),
                      v.rearrange("(a h) d -> a (h d)", a=1).partition_broadcast(P))
                     for m, v in enumerate((lq1, lk1, lq2, lk2))]
            small += [(rmscol[2 * DH * r:2 * DH * (r + 1), :], rms.rearrange("(n a) -> n a", a=1)) for r in range(P // (2 * DH))]
            small += [(ident[:, :], c_ident), (causalf[:, :], c_causal), (same[:, :], c_same), (before[:, :], c_before),
                      (wo[:, :, :], WoT.rearrange("(a p) n -> p a n", p=P)), (wg[:, :], Wg),
                      (w1[:, :, :], W1.rearrange("e p f -> p e f")),
                      (w2[:, :, :, :], W2.rearrange("e (a p) n -> p e a n", p=P)),
                      (x_tok[:, :, :], X.rearrange("b (t p) d -> p (b t) d", p=P))]
            for dst, src in small:
                sp.dma_start(dst, src).then_inc(s_w, 16)

            u = 0
            for b in range(B):
                for half in range(2):
                    for qk in range(2):
                        for t0 in (0, BANK):
                            sp.wait_ge(s_lo, u + 1)
                            for r in range(3):
                                f0 = (2 * b + half) * P
                                dst = parts_dram[qk, r, f0:f0 + P, t0:t0 + BANK]
                                sp.dma_start(dst, part_sb[u][:, r, :]).then_inc(s_stored, 16)
                            u += 1

            def load(g, buf):
                row, group, part = MAPS * N, MAPS * DH * N, G * MAPS * DH * N
                for r in range(3):
                    rows = slice(3 * r * DH, 3 * (r + 1) * DH)
                    q_src = bass.AP(parts_dram.tensor, g * group + r * part, [[0, 3], [row, DH], [1, row]])
                    k_src = bass.AP(parts_dram.tensor, g * group + 3 * part, [[part, 3], [row, DH], [1, row]])
                    sp.dma_start(q_op[buf][rows, :, :].rearrange("p c n -> p (c n)"), q_src).then_inc(s_load[buf], 16)
                    sp.dma_start(k_op[buf][rows, :, :].rearrange("p c n -> p (c n)"), k_src).then_inc(s_load[buf], 16)

                sp.dma_start(q_op[buf][ROWS:SROWS, :, :].rearrange("p c n -> p (c n)"),
                             q_op[buf][SROWS:SROWS + 2, :, :].rearrange("p c n -> p (c n)")).then_inc(s_load[buf], 16)

            def shift(n_done, buf):
                sp.wait_ge(s_afree, n_done)
                for r in range(2):
                    sp.dma_start(q_op[buf][ROWS + r:ROWS + r + 1, :, :].rearrange("a c (t q) -> a (c t) q", t=NT),
                                 mT[r * MAPS * NT:(r + 1) * MAPS * NT, :]).then_inc(s_shift, 16)

            sp.wait_ge(s_const, 1)
            sp.wait_ge(s_pool_const, 1)
            sp.wait_ge(s_stored, 48 * 16)
            load(0, 0)
            load(1, 1)
            shift(len(ALL_MAX) + 1, 0)

            def body(it, u, n):
                if n + 2 < G:
                    sp.wait_ge(s_bfree, it * (UNROLL * N_B) + (u * N_B + NRING))
                    load(it * UNROLL + (u + 2), (u + 2) % NBUF)
                if n + 1 < G:
                    shift(it * (UNROLL * N_A) + (a_before(n) - (n - u) * N_A + a_items(n).index(("shift", None)) + 1), (u + 1) % NBUF)

            body(0, 0, 0)
            with sp.Fori(0, LOOPS) as it:
                for u in range(1, UNROLL + 1):
                    body(it, u, u)
            for n in range(1 + LOOPS * UNROLL, G):
                body((n - 1) // UNROLL, (n - 1) % UNROLL + 1, n)

            for b in range(B):
                sp.wait_ge(s_final, b + 1)
                sp.dma_start(out[b, :, :].rearrange("(t p) d -> p t d", p=P),
                             y[:, b * NT:(b + 1) * NT, :]).then_inc(s_out, 16)
            sp.wait_ge(s_out, 16 * B)

        @block.gpsimd
        def _(pool):
            nc.gpsimd.memset(arena[64:P, NBUF * nq // 2:NBUF * nq].bitcast(I32), 0x3F803F80).then_inc(s_pool_const, 1)
            pool.wait_ge(s_pool_const, 1)
            nc.gpsimd.memset(v_grp[:, :, :, :, :], 0.0).then_inc(s_pool_const, 1)
            pool.wait_ge(s_pool_const, 2)
            nc.gpsimd.memset(v_grp[:, :, :, :, 2 * DH:2 * DH + 1], 1.0).then_inc(s_pool_const, 1)
            for e in range(E):
                nc.gpsimd.memset(order[:, e:e + 1], float(E - e)).then_inc(s_pool_const, 1)
            pool.wait_ge(s_pool_const, 3)
            pool.wait_ge(s_vcopy, TT)
            nc.gpsimd.tensor_copy(v_grp[:, 0, :, :, 0:2 * DH], v_all[:, 0, :, :, :]).then_inc(s_vgrp, 1)
            pool.wait_ge(s_const, 7)
            pool.sem_inc(s_ouse, 1)

            def waited(s, value):
                pool.wait_ge(s, value)
                pool.sem_inc(s_seen, 1)

            def normalise(it, u):
                slot, chain = it * UNROLL + u, it * (UNROLL * 3)
                waited(s_rinv, it * UNROLL + (u + 1))
                nc.gpsimd.tensor_tensor(out=o_norm[:, :, :, :].rearrange("p t c d -> p (t c) d"),
                                        in0=o_tr[:, :, :, 0:2 * DH].rearrange("p t c d -> p (t c) d"),
                                        in1=rinv[:, :, :].rearrange("p t c -> p (t c)").unsqueeze(2).broadcast_to([P, NT * MAPS, 2 * DH]),
                                        op=ALU.mult).then_inc(s_ochain, 1)
                waited(s_ochain, chain + (3 * u + 1))
                pool.sem_inc(s_ouse, 1)
                lam = nlam[:, bass.ds(slot, 1), :].rearrange("p a h -> p (a h)")
                for h in range(2):
                    last = nc.gpsimd.tensor_tensor(out=o_two[:, :, h, :], in0=o_norm[:, :, 2 * h + 1, :],
                                                   in1=lam[:, h:h + 1].unsqueeze(1).broadcast_to([P, NT, 2 * DH]), op=ALU.mult)
                last.then_inc(s_ochain, 1)
                waited(s_ochain, chain + (3 * u + 2))
                nc.gpsimd.tensor_tensor(out=o_all[:, bass.ds(slot, 1), :, :, :].rearrange("p a t h d -> p (a t) h d"),
                                        in0=o_norm[:, :, 0:MAPS:2, :], in1=o_two[:, :, :, :], op=ALU.add).then_inc(s_ochain, 1)

            def body(it, u, n):
                nb = it * (UNROLL * N_B)
                for s in range(NT):
                    slot = (u * NT + s) % NSLOT
                    waited(s_bfree, nb + (NRING + u * N_B + B_BEFORE[s + 1]))
                    nc.gpsimd.affine_select(out=probs[slot][:, :, 0:P], in_=probs[slot][:, :, 0:P], compare_op=ALU.is_ge,
                                            fill=0.0, base=0, pattern=[[0, MAPS], [1, P]],
                                            channel_multiplier=-1).then_inc(s_mask, 1)
                    if s == O_STEP + 1:
                        normalise(it, u)
                    if s == O_STEP + 2 and n + 1 < G:
                        nxt = it * UNROLL + (u + 1)
                        nc.gpsimd.tensor_copy(v_grp[:, (u + 1) % NBUF, :, :, 0:2 * DH].rearrange("p h t d -> p (h t) d"),
                                              v_all[:, bass.ds(nxt, 1), :, :, :].rearrange("p a h t d -> p (a h t) d")).then_inc(s_vgrp, 1)

            body(0, 0, 0)
            with pool.Fori(0, LOOPS) as it:
                for u in range(1, UNROLL + 1):
                    body(it, u, u)
            for n in range(1 + LOOPS * UNROLL, G):
                body((n - 1) // UNROLL, (n - 1) % UNROLL + 1, n)
            normalise(G // UNROLL, G % UNROLL)

        @block.scalar
        def _(act):
            def mid(u):
                act.wait_ge(s_rest, u + 1)
                nc.scalar.activation(part_sb[u][:, 1, :], rest[:, u % 2, :], ACT.Copy).then_inc(s_mid, 1)

            for u in range(16):
                act.wait_ge(s_proj, u + 1)
                nc.scalar.activation(part_sb[u][:, 0, :], bank[u % 6][:, :], ACT.Copy).then_inc(s_hi, 1)
                if u >= 1:
                    mid(u - 1)
            mid(15)
            for t in range(TT):
                act.wait_ge(s_vproj, t + 1)
                b, i = t // NT, t % NT
                nc.scalar.activation(v_all[:, b * GB:(b + 1) * GB, :, i, :],
                                     bank[t % 6][:, 0:2 * DH * H].rearrange("p (g h d) -> p g h d", g=GB, h=2),
                                     ACT.Copy).then_inc(s_vcopy, 1)
            act.wait_ge(s_const, 5)
            nc.scalar.activation(lexp[:, :, :], lsum[:, :, :], ACT.Exp).then_inc(s_lexp, 1)
            act.sem_inc(s_bfree, NRING)
            act.sem_inc(s_ocopy, 2)
            act.wait_ge(s_stored, 48 * 16)

            def copy_out(it, u):
                act.wait_ge(s_pfree, it * (UNROLL * NT) + (NSLOT + (u + 1) * NT))
                for half in range(2):
                    nc.scalar.activation(oT[:, half * BANK:(half + 1) * BANK], pv[half][:, :], ACT.Copy).then_inc(s_ocopy, 1)

            def out_transposed(it, u, half, idx):
                act.wait_ge(s_bfill, it * (UNROLL * N_B) + (idx + 1))
                nc.scalar.activation(o_tr[:, 4 * half:4 * half + 4, :, :].rearrange("p t c d -> p (t c d)"), ring_b[idx % NRING][:, :],
                                     ACT.Copy).then_inc(s_bfree, 1)

            def body(it, u, n):
                nb, n8 = it * (UNROLL * N_B), it * (UNROLL * NT)
                for s in range(NT):
                    slot = (u * NT + s) % NSLOT
                    act.wait_ge(s_pfree, n8 + (u * NT + s + 1))
                    for k, (kind, what) in enumerate(b_items(s)):
                        idx = u * N_B + B_BEFORE[s] + k
                        if kind == "out":
                            if what == 0:
                                act.wait_ge(s_ouse, it * UNROLL + (u + 1))
                            out_transposed(it, u, what, idx)
                            continue
                        _, c, a, z = what
                        act.wait_ge(s_bfill, nb + (idx + 1))
                        nc.scalar.activation(probs[slot][:, c, a - P * s:z - P * s], ring_b[idx % NRING][:, 0:z - a],
                                             ACT.Exp, scale=SCALE).then_inc(s_bfree, 1)
                    if s == COPY_STEP and u >= 1:
                        copy_out(it, u - 1)

            body(0, 0, 0)
            with act.Fori(0, LOOPS) as it:
                for u in range(1, UNROLL + 1):
                    body(it, u, u)
            for n in range(1 + LOOPS * UNROLL, G):
                body((n - 1) // UNROLL, (n - 1) % UNROLL + 1, n)
            copy_out((G - 1) // UNROLL, (G - 1) % UNROLL)
            act.wait_ge(s_ouse, G + 1)
            for half in range(2):
                out_transposed(G // UNROLL, G % UNROLL, half, (G % UNROLL) * N_B + half)

            act.wait_ge(s_ms, 1)
            nc.scalar.activation(ss[:, :], ss[:, :], ACT.Sqrt).then_inc(s_rms, 1)
            for t in range(TT):
                act.wait_ge(s_oct, t + 1)
                if t >= 2:
                    act.wait_ge(s_proj_o, t - 1)
                nc.scalar.activation(ocT[:, t % 2, :, :], bank[t % 2][:, 0:2 * D].rearrange("p (a n) -> p a n", a=2),
                                     ACT.Copy).then_inc(s_octc, 1)
            act.wait_ge(s_var, 1)
            nc.scalar.activation(rstd[:, :], rstd[:, :], ACT.Sqrt).then_inc(s_std, 1)
            for q in range(4):
                act.wait_ge(s_x1t, q + 1)
                nc.scalar.activation(xT[:, q * BANK:(q + 1) * BANK], bank[q][:, :], ACT.Copy).then_inc(s_x1tc, 1)
            act.wait_ge(s_lgsub, 1)
            nc.scalar.activation(key[:, :, :], pr[:, :, :], ACT.Exp).then_inc(s_lgexp, 1)
            for e in range(E):
                for f in range(2):
                    for q in range(4):
                        i = (e * 2 + f) * 4 + q
                        act.wait_ge(s_hid, i + 1)
                        if e >= HT_SLOTS:
                            act.wait_ge(s_y, 4 * (e - HT_SLOTS + 1))
                        nc.scalar.activation(hT[e % HT_SLOTS][:, f, q * BANK:(q + 1) * BANK], bank[5 + i % 3][:, :],
                                             ACT.Gelu).then_inc(s_gelu, 1)
            for b in range(B):
                act.wait_ge(s_var2, b + 1)
                nc.scalar.activation(rstd[:, b * NT:(b + 1) * NT], rstd[:, b * NT:(b + 1) * NT], ACT.Sqrt).then_inc(s_std2, 1)

        @block.vector
        def _(dve):
            nc.vector.memset(arena[64:P, 0:NBUF * nq // 2], 0.0).then_inc(s_const, 1)
            nc.vector.memset(oT[:, :], 1.0)
            nc.vector.memset(nlam[:, 0:1, :], 1.0)
            nc.vector.memset(m_parts[:, :, :], 0.0)
            nc.vector.memset(m_raw[:, :, :, :], -3.0e38).then_inc(s_const, 1)
            def low(u):
                dve.wait_ge(s_mid, u + 1)
                nc.vector.tensor_tensor(out=part_sb[u][:, 2, :], in0=rest[:, u % 2, :], in1=part_sb[u][:, 1, :],
                                        op=ALU.subtract).then_inc(s_lo, 1)

            for u in range(16):
                dve.wait_ge(s_hi, u + 1)
                if u >= 2:
                    dve.wait_ge(s_lo, u - 1)
                nc.vector.tensor_tensor(out=rest[:, u % 2, :], in0=bank[u % 6][:, :], in1=part_sb[u][:, 0, :],
                                        op=ALU.subtract).then_inc(s_rest, 1)
                if u >= 1:
                    low(u - 1)
            low(15)
            dve.wait_ge(s_w, 16 * N_SMALL)
            nc.vector.tensor_copy(identb[:, :], ident[:, :])
            nc.vector.tensor_copy(causalb[:, :], causalf[:, :]).then_inc(s_const, 1)
            nc.vector.tensor_tensor(out=lprod[:, :, :, :], in0=lvec[:, 0:4:2, :, :], in1=lvec[:, 1:4:2, :, :], op=ALU.mult).then_inc(s_const, 1)
            dve.wait_ge(s_const, 4)
            nc.vector.tensor_reduce(out=lsum[:, :, :], in_=lprod[:, :, :, :], axis=AX.X, op=ALU.add).then_inc(s_const, 1)
            dve.wait_ge(s_lexp, 1)
            for b in range(B):
                nc.vector.scalar_tensor_tensor(out=nlam[:, 1 + b * GB:1 + (b + 1) * GB, :].rearrange("p g h -> p (g h)"),
                                               in0=lexp[:, 1, :], scalar=-LAMBDA_INIT, in1=lexp[:, 0, :],
                                               op0=ALU.add, op1=ALU.subtract).then_inc(s_const, 1)
            dve.wait_ge(s_const, 7)

            def take_max(unit, idx):
                c, i, n, a, z = unit
                nc.vector.tensor_reduce(out=m_raw[:, c, i, n:n + 1], in_=ring_a[idx % NRING][:, 0:z - a],
                                        axis=AX.X, op=ALU.max).then_inc(s_afree, 1)

            def split_max(a_done, chain):
                dve.wait_ge(s_afree, a_done)
                nc.vector.tensor_reduce(out=m_neg[:, :], in_=m_raw[:, :, :, :].rearrange("p c t n -> p (c t) n"),
                                        axis=AX.X, op=ALU.max, negate=True).then_inc(s_mchain, 1)
                dve.wait_ge(s_mchain, chain + 1)
                nc.vector.tensor_copy(m_parts[:, 0, :], m_neg[:, :]).then_inc(s_mchain, 1)
                dve.wait_ge(s_mchain, chain + 2)
                nc.vector.tensor_tensor(out=m_parts[:, 1, :], in0=m_neg[:, :], in1=m_parts[:, 0, :],
                                        op=ALU.subtract).then_inc(s_mchain, 1)

            def copy_shift(idx, shifts):
                dve.wait_ge(s_shift, shifts)
                nc.vector.tensor_copy(mT[:, :], ring_a[idx % NRING][:, :].bitcast(BF16)[0:2 * MAPS * NT, 0:P]).then_inc(s_afree, 1)

            def invert_sums(it, u, b_done):
                dve.wait_ge(s_bfree, b_done)
                nc.vector.reciprocal(rinv[:, :, :], o_tr[:, :, :, 2 * DH]).then_inc(s_rinv, 1)

            idx = 0
            for _, unit in ALL_MAX:
                dve.wait_ge(s_afill, idx + 1)
                take_max(unit, idx)
                idx += 1
            split_max(idx, 0)
            dve.wait_ge(s_afill, idx + 1)
            copy_shift(idx, 0)
            idx += 1
            for _, unit in EARLY_MAX:
                dve.wait_ge(s_afill, idx + 1)
                take_max(unit, idx)
                idx += 1

            def body(it, u, n):
                na = it * (UNROLL * N_A)
                a = a_before(n) - (n - u) * N_A
                items = a_items(n)
                last_max = max((k for k, (kind, _) in enumerate(items) if kind == "max"), default=-1)
                for k, (kind, what) in enumerate(items):
                    dve.wait_ge(s_afill, na + (a + 1))
                    if kind == "shift":
                        copy_shift(a, it * (UNROLL * 32) + 32 * (u + 1))
                    else:
                        take_max(what, a)
                    a += 1
                    if k == last_max:
                        split_max(na + a, it * (UNROLL * 3) + 3 * (u + 1))
                    if k == INVERT_AT:
                        invert_sums(it, u, it * (UNROLL * N_B) + (u * N_B + OUT_AT + NRING))
                if len(items) <= INVERT_AT:
                    invert_sums(it, u, it * (UNROLL * N_B) + (u * N_B + OUT_AT + NRING))

            body(0, 0, 0)
            with dve.Fori(0, LOOPS) as it:
                for u in range(1, UNROLL + 1):
                    body(it, u, u)
            for n in range(1 + LOOPS * UNROLL, G):
                body((n - 1) // UNROLL, (n - 1) % UNROLL + 1, n)
            invert_sums(G // UNROLL, G % UNROLL, G * N_B + 2 + NRING)

            chain = [0]

            def link(ins):
                chain[0] += 1
                ins.then_inc(s_dchain, 1)
                dve.wait_ge(s_dchain, chain[0])

            V = nc.vector
            dve.wait_ge(s_ochain, 3 * (G + 1))
            link(V.tensor_tensor(out=o_sq, in0=o_flat, in1=o_flat, op=ALU.mult))
            link(V.tensor_reduce(out=ss[:, :], in_=o_sq, axis=AX.X, op=ALU.add))
            V.tensor_scalar(ss[:, :], ss[:, :], 1.0 / (2 * DH), EPS, ALU.mult, ALU.add).then_inc(s_ms, 1)
            link(V.tensor_scalar(wo[:, :, :], wo[:, :, :], rmscol[:, 0:1], 1.0 - LAMBDA_INIT, ALU.mult, ALU.mult))
            dve.wait_ge(s_rms, 1)
            link(V.reciprocal(ss[:, :], ss[:, :]))
            inv_rms = ss[:, :].rearrange("p (g t h) -> p g t h", g=G, t=NT)
            for b in range(B):
                for h in range(2):
                    gs = slice(b * GB, (b + 1) * GB)
                    last = V.tensor_tensor(out=o_tok[:, b * NT:(b + 1) * NT, :, h, :].rearrange("p t g d -> p g t d"),
                                           in0=o_all[:, 1 + b * GB:1 + (b + 1) * GB, :, h, :],
                                           in1=inv_rms[:, gs, :, h].unsqueeze(3).broadcast_to([P, GB, NT, 2 * DH]), op=ALU.mult)
            last.then_inc(s_onorm, 1)
            for t in range(TT):
                dve.wait_ge(s_proj_o, t + 1)
                V.tensor_tensor(out=x_tok[:, t, :], in0=bank[2 + t % 2][:, 0:D], in1=x_tok[:, t, :], op=ALU.add).then_inc(s_x1sum, 1)
                dve.wait_ge(s_x1sum, t + 1)
                link(V.bn_stats(stats[:, t, :], x_tok[:, t, :]))
                link(V.bn_aggr(mv[:, t, :], stats[:, t, :]))
            V.tensor_scalar(rstd[:, :], mv[:, :, 1], EPS, None, ALU.add).then_inc(s_var, 1)
            dve.wait_ge(s_std, 1)
            link(V.reciprocal(rstd[:, :], rstd[:, :]))
            for t in range(TT):
                last = V.tensor_scalar(x_tok[:, t, :], x_tok[:, t, :], mv[:, t, 0:1], rstd[:, t:t + 1], ALU.subtract, ALU.mult)
                if t % 4 == 3:
                    last.then_inc(s_x1, 1)

            def wide(x):
                return x.unsqueeze(2).broadcast_to([P, TT, E])

            dve.wait_ge(s_logit, 1)
            link(V.tensor_copy(lg[:, :, :], bank[4][:, 0:TT * E].rearrange("p (t e) -> p t e", e=E)))
            link(V.tensor_reduce(out=rt1[:, :], in_=lg[:, :, :], axis=AX.X, op=ALU.max))
            V.tensor_tensor(out=pr[:, :, :], in0=lg[:, :, :], in1=wide(rt1[:, :]), op=ALU.subtract).then_inc(s_lgsub, 1)
            dve.wait_ge(s_lgexp, 1)
            link(V.tensor_reduce(out=rt2[:, :], in_=key[:, :, :], axis=AX.X, op=ALU.add))
            link(V.reciprocal(rt2[:, :], rt2[:, :]))
            V.tensor_tensor(out=pr[:, :, :], in0=key[:, :, :], in1=wide(rt2[:, :]), op=ALU.mult).then_inc(s_prob, 1)
            dve.wait_ge(s_prt, 1)
            V.memset(cand[:, :], 1 << (N_BITS - 1))
            V.memset(ones[:, :], 1.0)
            link(V.tensor_copy(prT[:, :], bank[0][:, 0:P]))
            threshold = cand[:, 0:1].bitcast(F32)
            for k in range(N_BITS):
                bit, following = 1 << (N_BITS - 1 - k), (1 << (N_BITS - 1 - k)) >> 1
                V.tensor_scalar(cmp[:, :], prT[:, :], threshold, None, ALU.is_ge, ALU.add, accum_out=cnt[:, 0:1]).then_inc(s_count, 1)
                dve.wait_ge(s_total, k + 1)
                link(V.tensor_scalar(fail[:, :], bank[1][:, 0:1], float(CAP), float(bit), ALU.is_lt, ALU.mult))
                link(V.scalar_tensor_tensor(out=cand[:, :], in0=cand[:, :], scalar=following, in1=fail[:, :],
                                            op0=ALU.bitwise_xor, op1=ALU.bitwise_xor))
            link(V.tensor_scalar(cmp[:, :], prT[:, :], threshold, None, ALU.is_gt, ALU.add, accum_out=cnt[:, 0:1]))
            V.tensor_scalar(cmp2[:, :], prT[:, :], threshold, None, ALU.is_equal, ALU.add, accum_out=cnt[:, 1:2]).then_inc(s_tie, 1)
            dve.wait_ge(s_tie, 1)
            link(V.tensor_tensor_scan(out=scan[:, :], data0=ones[:, :], data1=cmp2[:, :], initial=0.0, op0=ALU.mult, op1=ALU.add))
            dve.wait_ge(s_tiesum, 1)
            link(V.tensor_scalar(need[:, :], bank[1][:, 8:9], -1.0, float(CAP), ALU.mult, ALU.add))
            link(V.tensor_tensor(out=need[:, :], in0=need[:, :], in1=bank[1][:, 16:17], op=ALU.subtract))
            link(V.scalar_tensor_tensor(out=cmp2[:, :], in0=scan[:, :], scalar=need[:, 0:1], in1=cmp2[:, :],
                                        op0=ALU.is_le, op1=ALU.mult))
            V.tensor_tensor(out=selT[:, :], in0=cmp[:, :], in1=cmp2[:, :], op=ALU.add).then_inc(s_selt, 1)
            dve.wait_ge(s_sel, 1)
            link(V.tensor_copy(sel[:, :, :], bank[2][:, 0:P].rearrange("p (t e) -> p t e", e=E)))
            link(V.tensor_reduce(out=rt1[:, :], in_=sel[:, :, :], axis=AX.X, op=ALU.max))
            link(V.tensor_scalar(rt1[:, :], rt1[:, :], -1.0, 1.0, ALU.mult, ALU.add))
            link(V.tensor_tensor(out=sel[:, :, :], in0=sel[:, :, :], in1=wide(rt1[:, :]), op=ALU.add))
            link(V.tensor_tensor(out=key[:, :, :], in0=pr[:, :, :], in1=sel[:, :, :], op=ALU.mult))
            link(V.scalar_tensor_tensor(out=key[:, :, :], in0=sel[:, :, :], scalar=-1.0, in1=key[:, :, :],
                                        op0=ALU.add, op1=ALU.add))
            link(V.tensor_reduce(out=rt2[:, :], in_=key[:, :, :], axis=AX.X, op=ALU.max))
            link(V.tensor_tensor(out=hit[:, :, :], in0=key[:, :, :], in1=wide(rt2[:, :]), op=ALU.is_equal))
            dve.wait_ge(s_pool_const, 3 + E)
            link(V.tensor_tensor(out=hit[:, :, :], in0=hit[:, :, :], in1=order[:, :].unsqueeze(1).broadcast_to([P, TT, E]),
                                 op=ALU.mult))
            link(V.tensor_reduce(out=rt1[:, :], in_=hit[:, :, :], axis=AX.X, op=ALU.max))
            link(V.tensor_tensor(out=hit[:, :, :], in0=hit[:, :, :], in1=wide(rt1[:, :]), op=ALU.is_equal))
            V.tensor_tensor(out=gate[:, :, :], in0=hit[:, :, :], in1=pr[:, :, :], op=ALU.mult).then_inc(s_gate, 1)
            dve.wait_ge(s_gate, 1)
            for e in range(E):
                for q in range(4):
                    dve.wait_ge(s_y, 4 * e + q + 1)
                    if e >= 1:
                        dve.wait_ge(s_yacc, 4 * (e - 1) + q + 1)
                    for t in range(4 * q, 4 * q + 4):
                        last = V.scalar_tensor_tensor(out=y[:, t, :], in0=bank[q][:, (t % 4) * D:(t % 4 + 1) * D],
                                                      scalar=gate[:, t, e:e + 1], in1=(y if e else x_tok)[:, t, :],
                                                      op0=ALU.mult, op1=ALU.add)
                    last.then_inc(s_yacc, 1)
            dve.wait_ge(s_yacc, 4 * E)
            for b in range(B):
                tiles = range(b * NT, (b + 1) * NT)
                for t in tiles:
                    last = V.bn_stats(stats[:, t, :], y[:, t, :])
                link(last)
                for t in tiles:
                    last = V.bn_aggr(mv[:, t, :], stats[:, t, :])
                link(last)
                V.tensor_scalar(rstd[:, b * NT:(b + 1) * NT], mv[:, b * NT:(b + 1) * NT, 1], EPS, None, ALU.add).then_inc(s_var2, 1)
            for b in range(B):
                dve.wait_ge(s_std2, b + 1)
                link(V.reciprocal(rstd[:, b * NT:(b + 1) * NT], rstd[:, b * NT:(b + 1) * NT]))
                for t in range(b * NT, (b + 1) * NT):
                    last = V.tensor_scalar(y[:, t, :], y[:, t, :], mv[:, t, 0:1], rstd[:, t:t + 1], ALU.subtract, ALU.mult)
                last.then_inc(s_final, 1)

        @block.tensor
        def _(pe):
            pe.wait_ge(s_x, 16 * 5)
            u = 0
            for b in range(B):
                for half in range(2):
                    for w in (wq, wk):
                        for t0 in (0, BANK):
                            if u >= 6:
                                pe.wait_ge(s_rest, u - 5)
                            nc.tensor.matmul(bank[u % 6][:, :], w[:, half * P:(half + 1) * P],
                                             xT[:, b * N + t0:b * N + t0 + BANK], start=True, stop=True).then_inc(s_proj, 1)
                            u += 1
            for t in range(TT):
                if t < 6:
                    pe.wait_ge(s_rest, 16)
                else:
                    pe.wait_ge(s_vcopy, t - 5)
                nc.tensor.matmul(bank[t % 6][:, 0:2 * DH * H], xT[:, t * P:(t + 1) * P], wv[:, :],
                                 start=True, stop=True).then_inc(s_vproj, 1)

            def max_unit(buf, unit, idx, free):
                c, i, n, a, z = unit
                if free is not None:
                    pe.wait_ge(s_afree, free)
                dst = ring_a[idx % NRING]
                masked = z == P * (i + 1)
                last = nc.tensor.matmul(dst[:, 0:z - a], q_op[buf][:, c, i * P:(i + 1) * P],
                                        k_op[buf][:, c, a:z], start=True, stop=not masked)
                if masked:
                    last = nc.tensor.matmul(dst[:, z - a - P:z - a], identb[:, :], causalb[:, :], start=False, stop=True)
                last.then_inc(s_afill, 1)

            def shift_unit(idx, chain, free):
                pe.wait_ge(s_mchain, chain)
                pe.wait_ge(s_afree, free)
                nc.tensor.transpose(ring_a[idx % NRING][:, :].bitcast(BF16)[:, 0:P],
                                    m_parts[:, :, :].rearrange("p r n -> p (r n)"), identb[:, :]).then_inc(s_afill, 1)

            def out_unit(half, idx, free):
                pe.wait_ge(s_bfree, free)
                for t in range(4):
                    last = nc.tensor.transpose(ring_b[idx % NRING][:, t * P:(t + 1) * P],
                                               oT[:, half * BANK + t * P:half * BANK + (t + 1) * P], ident[:, :])
                last.then_inc(s_bfill, 1)

            pe.wait_ge(s_const, 7)
            pe.wait_ge(s_vcopy, TT)
            pe.wait_ge(s_load[0], LOAD_INC)
            idx = 0
            for _, unit in ALL_MAX:
                max_unit(0, unit, idx, idx - 2 if idx >= NRING else None)
                idx += 1
            shift_unit(idx, 3, idx - 2)
            idx += 1
            pe.wait_ge(s_load[1], LOAD_INC)
            for _, unit in EARLY_MAX:
                max_unit(1, unit, idx, idx - 2)
                idx += 1

            def products(it, t, span):
                n8, u, s = it * (UNROLL * NT), t // NT, t % NT
                if s == 0:
                    pe.wait_ge(s_vgrp, it * UNROLL + (u + 1))
                    pe.wait_ge(s_ocopy, it * (UNROLL * 2) + 2 * (u + 1))
                pe.wait_ge(s_mask, n8 + (t + 1))
                a, z = span
                half = a // BANK
                for c in range(MAPS):
                    last = nc.tensor.matmul(pv[half][32 * c:32 * c + 32, a - half * BANK:z - half * BANK],
                                            v_grp[:, u % NBUF, c // 2, s, :],
                                            probs[t % NSLOT][:, c, a - P * s:z - P * s],
                                            start=s == 0, stop=s == (3 if half == 0 else 7))
                if z == N:
                    last.then_inc(s_pfree, 1)

            def body(it, u, n):
                na, nb = it * (UNROLL * N_A), it * (UNROLL * N_B)
                a, b_idx = a_before(n) - (n - u) * N_A, u * N_B
                pe.wait_ge(s_shift, it * (UNROLL * 32) + 32 * (u + 1))
                loaded = False
                for where, kind, what in pe_order(n):
                    if kind == "early" and not loaded:
                        pe.wait_ge(s_load[(u + 2) % NBUF], it * LOAD_INC + ((u + 2) // NBUF + 1) * LOAD_INC)
                        loaded = True
                    if kind == "score":
                        s, c, lo, hi = what
                        pe.wait_ge(s_bfree, nb + (b_idx + 1))
                        nc.tensor.matmul(ring_b[b_idx % NRING][:, 0:hi - lo], k_op[u % NBUF][:, c, s * P:(s + 1) * P],
                                         q_op[u % NBUF][:, c, lo:hi], start=True, stop=True).then_inc(s_bfill, 1)
                        b_idx += 1
                    elif kind == "out":
                        out_unit(what, b_idx, nb + (b_idx + 1))
                        b_idx += 1
                    elif where == "products":
                        products(it, u * NT + kind, what)
                    elif kind == "shift":
                        shift_unit(a, it * (UNROLL * 3) + 3 * (u + 2), na + (a - 2))
                        a += 1
                    else:
                        max_unit((u + (2 if kind == "early" else 1)) % NBUF, what, a, na + (a - 2))
                        a += 1

            pe.sem_inc(s_pfree, NSLOT)
            body(0, 0, 0)
            with pe.Fori(0, LOOPS) as it:
                for u in range(1, UNROLL + 1):
                    body(it, u, u)
            for n in range(1 + LOOPS * UNROLL, G):
                body((n - 1) // UNROLL, (n - 1) % UNROLL + 1, n)
            for t in range(G * NT - LAG, G * NT):
                for span in spans(P * (t % NT), N):
                    products(0, t, span)
            pe.wait_ge(s_ocopy, 2 * (G + 1))
            for half in range(2):
                b_idx = (G % UNROLL) * N_B + half
                out_unit(half, b_idx, (G // UNROLL) * UNROLL * N_B + b_idx + 1)

            def project(t):
                pe.wait_ge(s_octc, t + 1)
                if t >= 2:
                    pe.wait_ge(s_x1sum, t - 1)
                for a in range(2):
                    last = nc.tensor.matmul(bank[2 + t % 2][:, 0:D], ocT[:, t % 2, a, :], wo[:, a, :], start=a == 0, stop=a == 1)
                last.then_inc(s_proj_o, 1)

            pe.wait_ge(s_onorm, 1)
            for t in range(TT):
                if t >= 2:
                    pe.wait_ge(s_octc, t - 1)
                for a in range(2):
                    last = nc.tensor.transpose(bank[t % 2][:, a * P:(a + 1) * P],
                                               o_tok[:, t, 4 * a:4 * a + 4, :, :].rearrange("p g h d -> p (g h d)"), ident[:, :])
                last.then_inc(s_oct, 1)
                if t >= 1:
                    project(t - 1)
            project(TT - 1)
            for q in range(4):
                pe.wait_ge(s_x1, q + 1)
                for t in range(4):
                    last = nc.tensor.transpose(bank[q][:, t * P:(t + 1) * P], x_tok[:, 4 * q + t, :], ident[:, :])
                last.then_inc(s_x1t, 1)
            for t in range(TT):
                if t % 4 == 0:
                    pe.wait_ge(s_x1tc, t // 4 + 1)
                last = nc.tensor.matmul(bank[4][:, t * E:(t + 1) * E], xT[:, t * P:(t + 1) * P], wg[:, :], start=True, stop=True)
            last.then_inc(s_logit, 1)

            def hidden(i):
                e, f, q = i // 8, i // 4 % 2, i % 4
                if i >= 3:
                    pe.wait_ge(s_gelu, i - 2)
                nc.tensor.matmul(bank[5 + i % 3][:, :], w1[:, e, f * P:(f + 1) * P], xT[:, q * BANK:(q + 1) * BANK],
                                 start=True, stop=True).then_inc(s_hid, 1)

            def expert_out(e):
                pe.wait_ge(s_gelu, 8 * (e + 1))
                for q in range(4):
                    if e >= 1:
                        pe.wait_ge(s_yacc, 4 * (e - 1) + q + 1)
                    for t in range(4):
                        for f in range(2):
                            last = nc.tensor.matmul(bank[q][:, t * D:(t + 1) * D],
                                                    hT[e % HT_SLOTS][:, f, (4 * q + t) * P:(4 * q + t + 1) * P],
                                                    w2[:, e, f, :], start=f == 0, stop=f == 1)
                    last.then_inc(s_y, 1)

            for i in range(8 * HT_SLOTS):
                hidden(i)
                if i == 4:
                    pe.wait_ge(s_prob, 1)
                    nc.tensor.transpose(bank[0][:, 0:P], pr[:, :, :].rearrange("p t e -> p (t e)"), ident[:, :]).then_inc(s_prt, 1)
                if 5 <= i < 5 + N_BITS:
                    pe.wait_ge(s_count, i - 4)
                    nc.tensor.matmul(bank[1][:, 0:1], same[:, :], cnt[:, 0:1], start=True, stop=True).then_inc(s_total, 1)
                if i == 5 + N_BITS + 1:
                    pe.wait_ge(s_tie, 1)
                    nc.tensor.matmul(bank[1][:, 8:9], same[:, :], cnt[:, 0:1], start=True, stop=True)
                    nc.tensor.matmul(bank[1][:, 16:17], before[:, :], cnt[:, 1:2], start=True, stop=True).then_inc(s_tiesum, 1)
                if i == 5 + N_BITS + 3:
                    pe.wait_ge(s_selt, 1)
                    nc.tensor.transpose(bank[2][:, 0:P], selT[:, :], ident[:, :]).then_inc(s_sel, 1)
            pe.wait_ge(s_gate, 1)
            for e in range(E):
                expert_out(e)
                if HT_SLOTS + e < E:
                    for i in range(8 * (HT_SLOTS + e), 8 * (HT_SLOTS + e + 1)):
                        hidden(i)


_INS = ["X", "XT", "WqT", "WkT", "WvT", "WoT", "lq1", "lk1", "lq2", "lk2", "rms", "Wg", "W1", "W2",
        "c_ident", "c_causal", "c_same", "c_before"]


def kernel(**inputs):
    import numpy as np
    import concourse.bacc as bacc
    from concourse.bass_utils import run_bass_kernel_spmd

    x = np.asarray(inputs["L0_attn_X"])
    arrays = {"X": x, "XT": x.reshape(T, D).T}
    for n in ("Wq", "Wk", "Wv", "Wo"):
        arrays[n + "T"] = np.asarray(inputs[f"L0_attn_{n}"]).T
    for n in ("WqT", "WkT"):
        arrays[n] = arrays[n].reshape(D, GB, MAPS, DH).transpose(0, 1, 3, 2).reshape(D, 2 * DH * H)
    for n in ("lq1", "lk1", "lq2", "lk2"):
        arrays[n] = inputs[f"L0_attn_{n}"]
    arrays["rms"] = inputs["L0_attn_rms_scale"]
    for n in ("Wg", "W1", "W2"):
        arrays[n] = inputs[f"L0_ffn_{n}"]
    p = np.arange(P)
    same_expert = (p[:, None] - p[None, :]) % E == 0
    arrays["c_ident"] = np.eye(P, dtype=np.float32)
    arrays["c_causal"] = np.where(p[None, :] > p[:, None], np.float32(-1e30), np.float32(0))
    arrays["c_same"] = same_expert.astype(np.float32)
    arrays["c_before"] = (same_expert & (p[:, None] < p[None, :])).astype(np.float32)

    nc = bacc.Bacc("TRN2", target_bir_lowering=False, num_devices=1)
    ins = {f"in_{n}": np.ascontiguousarray(arrays[n]) for n in _INS}
    args = [nc.dram_tensor(n, a.shape, mybir.dt.from_np(a.dtype), kind="ExternalInput").ap() for n, a in ins.items()]
    args.append(nc.dram_tensor("out", (B, N, D), F32, kind="ExternalOutput").ap())
    build(nc, *args)
    return run_bass_kernel_spmd(nc, [ins], core_ids=[0]).results[0]["out"]
```

```python
from contextlib import ExitStack

import concourse.bass as bass
from concourse import mybir

ALU = mybir.AluOpType
ACT = mybir.ActivationFunctionType
AX = mybir.AxisListType
F32 = mybir.dt.float32
BF16 = mybir.dt.bfloat16
I32 = mybir.dt.int32

B, N, D = 2, 1024, 128
H, DH = 16, 8
E, F = 8, 256
T = B * N
CAP = T // E
LAMBDA_INIT, EPS = 0.8, 1e-5
SCALE = float(DH) ** -0.5

P = 128
BANK = 512
NT = N // P
TT = T // P
MAPS = 4
GB = 2 * H // MAPS
G = B * GB
ROWS = 9 * DH
SROWS = ROWS + 2
NBUF = 3
NRING = 3
NSLOT = 3
UNROLL = NBUF
LOOPS = (G - 3) // UNROLL

MAX_FIRST, MAX_EARLY = [7, 6, 4, 5], [0, 3, 1, 2]
DIAGONALS = MAX_FIRST + MAX_EARLY
NDIAG = 4
INVERT_AFTER = 2
SHIFT_LAG = 3
COPY_STEP = 0
LATENCY, MASK_TIME, DIAG_TIME = 450, 5500, 5500
MAX_COST, EXP_COST, PRODUCT_COST = (2.5, 250), (2, 120), 4.7
PACE = 1.2
FAR = 1 << 30
LAG = 2
O_STEP = 1


def spans(lo, hi):
    out = []
    while lo < hi:
        end = min(hi, (lo // BANK + 1) * BANK)
        out.append((lo, end))
        lo = end
    return out


LOAD_INC = 7 * 16
N_SMALL = P // (2 * DH) + 9
N_QK = B * 2 * 2 * 2
N_EARLY_QK = 4
N_PROJ = N_QK + TT
PROJ_BANKS = 5
PROJ_FIRST = 9
N_BITS = 30
SEARCH = N_BITS // 2
QUADS = TT // 4
HALF_Q = QUADS // B
N_HID = E * 2 * QUADS
Y_SOON = 1
Y_BANKS = [3, 4, 0, 5, 6, 7]


def max_units(tiles):
    out = []
    for i in tiles:
        for n, (a, z) in enumerate(spans(0, P * i)):
            maps = max(1, 1 << (BANK // (z - a)).bit_length() - 1)
            out += [(i, n, c, c + min(maps, MAPS), a, z) for c in range(0, MAPS, min(maps, MAPS))]
    return out


def diagonal_unit(i):
    return (i, 2, 0, MAPS, P * i, P * (i + 1))


def has_diagonal(d, n):
    return n + (1 if d < len(MAX_FIRST) else 2) < G


def a_items(n):
    items = [("max", x) for x in max_units(MAX_FIRST)] if n + 1 < G else []
    done = len(items)
    if n + 2 < G:
        items += [("early", x) for x in max_units(MAX_EARLY)]
    if n + 1 < G:
        items.insert(min(done + SHIFT_LAG, len(items)), ("shift", None))
    return items


def b_items(step, n):
    items = [("diagonal", step)] if has_diagonal(step, n) else []
    items += [("score", (step, c, a, z)) for c in range(MAPS) for a, z in spans(P * step, N)]
    if step == O_STEP:
        items += [("out", 0), ("out", 1)]
    return items


def b_before(n, step=0):
    return sum(len(b_items(s, m)) for m in range(n) for s in range(NT)) + sum(len(b_items(s, n)) for s in range(step))


def a_before(n):
    return FIRST_A + sum(len(a_items(m)) for m in range(n))


FIRST_BATCH = [(0.3, "heads", 0), (0.35, "heads", 1), (0.4, "project", 0), (0.45, "project", 1),
               (0.7, "x1", 0), (0.75, "x1", 1), (0.95, "logits", 0), (0.97, "logits", 1)]


def late_order():
    steps = {15: [("heads", 2), ("heads", 3)], 17: [("project", 2), ("project", 3)], 25: [("x1", 2), ("x1", 3)],
             26: [("logits", 2), ("logits", 3), ("exp", 1)], 31: [("probs", 0)]}
    order, searched = [], 0
    for i in range(N_HID):
        order.append(("hidden", i))
        order += steps.get(i, [])
        if i >= N_HID // 2 + 1 and i % 2 and searched < SEARCH:
            order.append(("search", searched))
            searched += 1
    order += [("search", k) for k in range(searched, SEARCH)]
    return order + [("ties", 0), ("y", 0), ("picked", 0)] + [("y", i) for i in range(1, Y_SOON)]


def pe_order(n):
    scores = [x for s in range(NT) for x in b_items(s, n)]
    maxima = a_items(n)
    first = -LAG if n else 0
    products = [(t, span) for t in range(first, NT - LAG) for span in spans(P * (t % NT), N)]
    a_done, b_done, masked = [0] * NRING, [0] * NRING, dict.fromkeys(range(-LAG, 0), MASK_TIME)

    def columns(kind, what):
        if kind in ("shift", "out", "diagonal"):
            return BANK
        return (what[-1] - what[-2]) * (what[3] - what[2] if kind in ("max", "early") else 1)

    def pe_cost(kind, what):
        return columns(kind, what) * (2 if kind in ("shift", "out") else 1)

    def reader_cost(kind, what, rate, fixed):
        return rate * columns(kind, what) + fixed

    work = sum(pe_cost(*x) for x in scores + maxima) + sum(PRODUCT_COST * (z - a) for _, (a, z) in products)
    pace = PACE * work / max(1, sum(reader_cost(*x, *MAX_COST) for x in maxima + [x for x in scores if x[0] == "diagonal"]))
    order, vector, now, due = [], [], 0, 0
    drained = None if n else 0
    copied = n == 0
    while scores or maxima or products:
        t_a = max(now, a_done[-NRING] + LATENCY) if maxima else FAR
        t_b = max(now, b_done[-NRING] + LATENCY) if scores else FAR
        if not copied and drained is not None and COPY_STEP in masked:
            b_done[-1] = max(b_done[-1], drained + LATENCY) + 4 * BANK
            masked[0] = max(masked[0], b_done[-1] + LATENCY)
            copied = True
        t_p = max(now, masked.get(products[0][0], FAR)) if products else FAR
        if products and products[0][0] == 0 and not copied:
            t_p = FAR
        if scores and scores[0][0] == "score" and products and products[0][0] <= scores[0][1][0] - NSLOT:
            t_b = FAR
        if t_a <= now and due <= now:
            pick = "a"
        elif t_b <= now:
            pick = "b"
        elif t_p <= now:
            pick = "products"
        else:
            now = min(t_a, t_b, t_p)
            pick = "a" if t_a == now else "b" if t_b == now else "products"
        if pick == "a":
            x = maxima.pop(0)
            now += pe_cost(*x)
            took = reader_cost(*x, *MAX_COST)
            vector.append((max(now + LATENCY, a_done[-1]), *x))
            a_done.append(max(now + LATENCY, a_done[-1]) + took)
            due += took * pace
            order.append(("a", *x))
        elif pick == "b":
            x = scores.pop(0)
            now += pe_cost(*x)
            b_done.append(max(now + LATENCY, b_done[-1]) + reader_cost(*x, *EXP_COST))
            order.append(("b", *x))
            if x[0] == "diagonal":
                due += reader_cost(*x, *MAX_COST) * pace
                vector.append((b_done[-1] + DIAG_TIME, *x))
            elif x[0] == "score" and (not scores or scores[0][0] != "score" or scores[0][1][0] > x[1][0]):
                masked[x[1][0]] = b_done[-1] + MASK_TIME
        else:
            t, (a, z) = products.pop(0)
            now += PRODUCT_COST * (z - a)
            order.append(("products", t, (a, z)))
            drained = now if t == -1 else drained
    vector = [x[1:] for x in sorted(vector, key=lambda x: x[0])]
    at = max((k for k, x in enumerate(vector) if x[0] == "max"), default=0)
    late = [x for x in vector[at + 1:] if x[0] == "diagonal" and x[1] < len(MAX_FIRST)]
    soon = [x for x in vector[:at] if x[0] == "diagonal" and x[1] >= len(MAX_FIRST)]
    vector = [x for x in vector[:at] if x not in soon] + late + vector[at:at + 1] + soon + [x for x in vector[at + 1:] if x not in late]
    return order, vector


N_B = b_before(1)
N_A = len(a_items(0))
FIRST_UNITS = [diagonal_unit(i) for i in MAX_FIRST + MAX_EARLY] + max_units(MAX_FIRST + MAX_EARLY)
EARLY_UNITS = [diagonal_unit(i) for i in MAX_EARLY] + max_units(MAX_EARLY)
FIRST_A = len(FIRST_UNITS) + 1 + len(EARLY_UNITS)
assert UNROLL * N_A % NRING == 0 and UNROLL * N_B % NRING == 0 and UNROLL * NT % NDIAG == 0 and UNROLL * NT % NSLOT == 0


def build(nc, X, XT, WqT, WkT, WvT, WoT, lq1, lk1, lq2, lk2, rms, Wg, W1, W2, c_ident, c_causal, c_same, c_before,
          c_weight, c_step, out):
    parts_dram = nc.dram_tensor("parts", (2, 3, G * MAPS * DH, N), BF16).ap()

    ctx = ExitStack()
    with ctx:
        def sb(name, shape, dt=F32):
            return ctx.enter_context(nc.sbuf_tensor(name, shape, dt))

        def sem(name):
            return ctx.enter_context(nc.semaphore(name))

        x_tok = sb("x_tok", [P, TT, D])
        xT = sb("xT", [P, T])
        wq, wk, wv = (sb(n, [P, 2 * DH * H]) for n in ("wq", "wk", "wv"))
        wo = sb("wo", [P, 2, D])
        wg = sb("wg", [P, E])
        w1 = sb("w1", [P, E, F])
        w2 = sb("w2", [P, E, 2, D])
        ident = sb("ident", [P, P])
        identb = sb("identb", [P, P], BF16)
        causalf = sb("causalf", [P, P])
        causalb = sb("causalb", [P, P], BF16)
        same = sb("same", [P, P])
        before = sb("before", [P, P])
        lvec = sb("lvec", [P, 4, H, DH])
        lprod = sb("lprod", [P, 2, H, DH])
        lsum = sb("lsum", [P, 2, H])
        lexp = sb("lexp", [P, 2, H])
        nlam = sb("nlam", [P, G + 1, 2])
        rmscol = sb("rmscol", [P, 1])
        arena = sb("arena", [P, E * 2 * T])
        a_b = arena[:, :].bitcast(BF16)
        nq = MAPS * N
        q_op = [a_b[:, u * nq:(u + 1) * nq].rearrange("p (c n) -> p c n", c=MAPS) for u in range(NBUF)]
        k_op = [a_b[:, (NBUF + u) * nq:(NBUF + u + 1) * nq].rearrange("p (c n) -> p c n", c=MAPS) for u in range(NBUF)]
        p_at = NBUF * nq
        probs = [arena[:, p_at + s * nq:p_at + (s + 1) * nq].rearrange("p (c n) -> p c n", c=MAPS) for s in range(NSLOT)]
        pa = 2 * p_at
        part_sb = [a_b[:, pa + u * 3 * BANK:pa + (u + 1) * 3 * BANK].rearrange("p (r n) -> p r n", r=3) for u in range(N_QK)]
        hT = [arena[:, e * 2 * T:(e + 1) * 2 * T].rearrange("p (f n) -> p f n", f=2) for e in range(E)]
        late_at, v_at = 6 * 2 * T, 7 * 2 * T
        rest = sb("rest", [P, NDIAG, BANK])
        v_all = arena[:, v_at:v_at + G * 2 * NT * 2 * DH].rearrange("p (g h t d) -> p g h t d", g=G, h=2, t=NT)
        oT = arena[:, late_at:late_at + N]
        o_all = sb("o_all", [P, G + 1, NT, 2, 2 * DH])
        block_sb = o_all[:, 0:12, :, :, :].rearrange("p g t h d -> p (g t h d)").rearrange("p (r n) -> p r n", n=BANK)
        tr_at = late_at + N
        o_tr = arena[:, tr_at:tr_at + NT * MAPS * 32].rearrange("p (t c d) -> p t c d", t=NT, c=MAPS)
        grp_at = tr_at + NT * MAPS * 32
        v_grp = arena[:, grp_at:grp_at + NBUF * 2 * NT * 32].rearrange("p (u h t d) -> p u h t d", u=NBUF, h=2, t=NT)
        norm_at = grp_at + NBUF * 2 * NT * 32
        o_norm = arena[:, norm_at:norm_at + NT * MAPS * 2 * DH].rearrange("p (t c d) -> p t c d", t=NT, c=MAPS)
        rinv = sb("rinv", [P, NT, MAPS])
        o_two = sb("o_two", [P, NT, 2, 2 * DH])
        m_raw = sb("m_raw", [P, MAPS, NT, 3])
        m_neg = sb("m_neg", [P, MAPS * NT])
        m_parts = sb("m_parts", [P, 4, MAPS * NT], BF16)
        mT = sb("mT", [2 * MAPS * NT, P], BF16)
        ss = sb("ss", [P, G * NT * 2])
        stats = sb("stats", [P, TT, 6])
        mv = sb("mv", [P, TT, 2])
        rstd = sb("rstd", [P, TT])
        guess = sb("guess", [P, GB * NT * 2])
        step = sb("step", [P, GB * NT * 2])
        lg = sb("lg", [P, TT, E])
        pr = sb("pr", [P, TT, E])
        rt1 = sb("rt1", [P, TT])
        rt2 = sb("rt2", [P, TT])
        sel = sb("sel", [P, TT, E])
        key = sb("key", [P, TT, E])
        hit = sb("hit", [P, TT, E])
        order = sb("order", [P, E])
        gate = sb("gate", [P, TT, E])
        prT = sb("prT", [P, P])
        cmp = sb("cmp", [P, 3, P])
        cmp2 = sb("cmp2", [P, P])
        scan = sb("scan", [P, P])
        cnt = sb("cnt", [P, 3])
        cand = sb("cand", [P, 3], I32)
        met = sb("met", [P, 3], I32)
        bits = sb("bits", [P, 1], I32)
        weight = sb("weight", [P, SEARCH, 3])
        change = sb("change", [P, SEARCH + 1, 3], I32)
        need = sb("need", [P, 1])
        selT = sb("selT", [P, P])
        ones = sb("ones", [P, P])
        width = GB * NT * 2 * 2 * DH
        sq_at, tok_at, oct_at = (2048, v_at), (NBUF * 2048 + 2048, v_at + width), (2 * 2048, late_at)
        o_tok = [arena[:, at:at + width].rearrange("p (t g h d) -> p t g h d", t=NT, g=GB, h=2) for at in tok_at]
        ocT = [arena[:, at:at + width].rearrange("p (q t a n) -> p q t a n", q=HALF_Q, t=4, a=2) for at in oct_at]
        y = o_all[:, 0:8, :, :, :].rearrange("p g t h d -> p (g t h d)").rearrange("p (t d) -> p t d", d=D)

        bank = [ctx.enter_context(nc.psum_tensor(f"bank{i}", [P, BANK], F32)) for i in range(8)]
        ring_a, ring_b, pv = bank[0:3], bank[3:6], bank[6:8]

        s_x = sem("s_x")
        s_x2 = sem("s_x2")
        s_masks = sem("s_masks")
        s_lam = sem("s_lam")
        s_w = sem("s_w")
        s_const = sem("s_const")
        s_pool_const = sem("s_pool_const")
        s_proj = sem("s_proj")
        s_hi = sem("s_hi")
        s_rest = sem("s_rest")
        s_mid = sem("s_mid")
        s_lo = sem("s_lo")
        s_block = sem("s_block")
        s_brest = sem("s_brest")
        s_bmid = sem("s_bmid")
        s_blo = sem("s_blo")
        s_stored = sem("s_stored")
        s_vproj = sem("s_vproj")
        s_vcopy = sem("s_vcopy")
        s_vgrp = sem("s_vgrp")
        s_load = [sem(f"s_load{u}") for u in range(NBUF)]
        s_afill = sem("s_afill")
        s_dmask = sem("s_dmask")
        s_dused = sem("s_dused")
        s_afree = sem("s_afree")
        s_bfill = sem("s_bfill")
        s_bfree = sem("s_bfree")
        s_seen = sem("s_seen")
        s_mask = sem("s_mask")
        s_pfree = sem("s_pfree")
        s_ocopy = sem("s_ocopy")
        s_mchain = sem("s_mchain")
        s_shift = sem("s_shift")
        s_ouse = sem("s_ouse")
        s_rinv = sem("s_rinv")
        s_ochain = sem("s_ochain")
        s_lexp = sem("s_lexp")
        s_dchain = sem("s_dchain")
        s_onorm = sem("s_onorm")
        s_oct = sem("s_oct")
        s_octc = sem("s_octc")
        s_proj_o = sem("s_proj_o")
        s_x1sum = sem("s_x1sum")
        s_x1 = sem("s_x1")
        s_x1t = sem("s_x1t")
        s_x1tc = sem("s_x1tc")
        s_logit = sem("s_logit")
        s_lgsub = sem("s_lgsub")
        s_lgexp = sem("s_lgexp")
        s_prob = sem("s_prob")
        s_prt = sem("s_prt")
        s_count = sem("s_count")
        s_total = sem("s_total")
        s_tie = sem("s_tie")
        s_tiesum = sem("s_tiesum")
        s_selt = sem("s_selt")
        s_sel = sem("s_sel")
        s_gate = sem("s_gate")
        s_hid = sem("s_hid")
        s_gelu = sem("s_gelu")
        s_y = sem("s_y")
        s_yacc = sem("s_yacc")
        s_var = sem("s_var")
        s_std = sem("s_std")
        s_final = sem("s_final")
        s_out = sem("s_out")

        block = ctx.enter_context(nc.Block())

        def heads_bank(q):
            return 3 if q == 3 else 0

        def project_bank(q):
            return 0 if q == 3 else 2

        def x1_bank(q):
            return q % HALF_Q + q // HALF_Q

        def logits_bank(q):
            return 2 + q // HALF_Q

        @block.sync
        def _(sp):
            sp.dma_start(xT[:, 0:BANK], XT[:, 0:BANK]).then_inc(s_x, 16)
            sp.dma_start(wq[:, :], WqT).then_inc(s_x, 16)
            sp.dma_start(xT[:, BANK:N], XT[:, BANK:N]).then_inc(s_x, 16)
            sp.dma_start(xT[:, N:T], XT[:, N:T]).then_inc(s_x2, 16)
            sp.dma_start(wv[:, :], WvT).then_inc(s_x2, 16)

            def store(u):
                b, half, qk, t0 = u // 8, u // 4 % 2, u // 2 % 2, u % 2 * BANK
                f0 = (2 * b + half) * P
                sp.dma_start(parts_dram[qk, :, f0:f0 + P, t0:t0 + BANK].rearrange("r p n -> p r n"),
                             part_sb[u][:, :, :]).then_inc(s_stored, 16)

            def load(g, buf):
                row, group, part = MAPS * N, MAPS * DH * N, G * MAPS * DH * N
                for r in range(3):
                    rows = slice(3 * r * DH, 3 * (r + 1) * DH)
                    q_src = bass.AP(parts_dram.tensor, g * group + r * part, [[0, 3], [row, DH], [1, row]])
                    k_src = bass.AP(parts_dram.tensor, g * group + 3 * part, [[part, 3], [row, DH], [1, row]])
                    sp.dma_start(q_op[buf][rows, :, :].rearrange("p c n -> p (c n)"), q_src).then_inc(s_load[buf], 16)
                    sp.dma_start(k_op[buf][rows, :, :].rearrange("p c n -> p (c n)"), k_src).then_inc(s_load[buf], 16)

                sp.dma_start(q_op[buf][ROWS:SROWS, :, :].rearrange("p c n -> p (c n)"),
                             q_op[buf][SROWS:SROWS + 2, :, :].rearrange("p c n -> p (c n)")).then_inc(s_load[buf], 16)

            def shift(n_done, buf):
                sp.wait_ge(s_afree, n_done)
                for r in range(2):
                    sp.dma_start(q_op[buf][ROWS + r:ROWS + r + 1, :, :].rearrange("a c (t q) -> a (c t) q", t=NT),
                                 mT[r * MAPS * NT:(r + 1) * MAPS * NT, :]).then_inc(s_shift, 16)

            sp.wait_ge(s_const, 1)
            sp.wait_ge(s_pool_const, 1)
            for u in range(N_EARLY_QK):
                sp.wait_ge(s_lo, u + 1)
                store(u)
            sp.wait_ge(s_stored, N_EARLY_QK * 16)
            load(0, 0)
            load(1, 1)
            for u in range(N_EARLY_QK, N_QK):
                sp.wait_ge(s_blo, u - N_EARLY_QK + 1)
                store(u)
            shift(len(FIRST_UNITS) + 1 + SHIFT_LAG, 0)
            sp.wait_ge(s_stored, N_QK * 16)

            small = [(rmscol[2 * DH * r:2 * DH * (r + 1), :], rms.rearrange("(n a) -> n a", a=1)) for r in range(P // (2 * DH))]
            small += [(same[:, :], c_same), (before[:, :], c_before),
                      (wo[:, :, :], WoT.rearrange("(a p) n -> p a n", p=P)), (wg[:, :], Wg),
                      (w1[:, :, :], W1.rearrange("e p f -> p e f")),
                      (w2[:, :, :, :], W2.rearrange("e (a p) n -> p e a n", p=P)),
                      (x_tok[:, :, :], X.rearrange("b (t p) d -> p (b t) d", p=P)),
                      (weight[:, :, :], c_weight.unsqueeze(0).partition_broadcast(P)),
                      (change[:, :, :], c_step.unsqueeze(0).partition_broadcast(P))]
            for dst, src in small:
                sp.dma_start(dst, src).then_inc(s_w, 16)

            def body(it, u, n):
                if n + 2 < G:
                    sp.wait_ge(s_bfree, it * (UNROLL * N_B) + (b_before(n) - (n - u) * N_B + NRING))
                    load(it * UNROLL + (u + 2), (u + 2) % NBUF)
                if n + 1 < G:
                    shift(it * (UNROLL * N_A) + (a_before(n) - (n - u) * N_A + a_items(n).index(("shift", None)) + 1), (u + 1) % NBUF)

            body(0, 0, 0)
            with sp.Fori(0, LOOPS) as it:
                for u in range(1, UNROLL + 1):
                    body(it, u, u)
            for n in range(1 + LOOPS * UNROLL, G):
                body((n - 1) // UNROLL, (n - 1) % UNROLL + 1, n)

            for q in range(QUADS):
                sp.wait_ge(s_final, q + 1)
                b, n0 = q // HALF_Q, q % HALF_Q * BANK
                sp.dma_start(out[b, n0:n0 + BANK, :].rearrange("(t p) d -> p t d", p=P),
                             y[:, 4 * q:4 * q + 4, :]).then_inc(s_out, 16)
            sp.wait_ge(s_out, 16 * QUADS)

        @block.gpsimd
        def _(pool):
            nc.gpsimd.memset(arena[64:P, NBUF * nq // 2:NBUF * nq].bitcast(I32), 0x3F803F80).then_inc(s_pool_const, 1)
            pool.wait_ge(s_pool_const, 1)
            nc.gpsimd.memset(v_grp[:, :, :, :, :], 0.0).then_inc(s_pool_const, 1)
            pool.wait_ge(s_pool_const, 2)
            nc.gpsimd.memset(v_grp[:, :, :, :, 2 * DH:2 * DH + 1], 1.0).then_inc(s_pool_const, 1)
            for e in range(E):
                nc.gpsimd.memset(order[:, e:e + 1], float(E - e)).then_inc(s_pool_const, 1)
            pool.wait_ge(s_pool_const, 3)

            def block_low(k):
                pool.wait_ge(s_bmid, k + 1)
                nc.gpsimd.tensor_tensor(out=part_sb[N_EARLY_QK + k][:, 2, :], in0=block_sb[:, k % 6, :],
                                        in1=part_sb[N_EARLY_QK + k][:, 1, :], op=ALU.subtract).then_inc(s_blo, 1)

            for k in range(N_QK - N_EARLY_QK):
                pool.wait_ge(s_block, k + 1)
                nc.gpsimd.tensor_tensor(out=block_sb[:, k % 6, :], in0=block_sb[:, k % 6, :],
                                        in1=part_sb[N_EARLY_QK + k][:, 0, :], op=ALU.subtract).then_inc(s_brest, 1)
                if k >= 1:
                    block_low(k - 1)
            block_low(N_QK - N_EARLY_QK - 1)
            pool.wait_ge(s_vcopy, TT)
            nc.gpsimd.tensor_copy(v_grp[:, 0, :, :, 0:2 * DH], v_all[:, 0, :, :, :]).then_inc(s_vgrp, 1)
            pool.wait_ge(s_const, 7)
            pool.sem_inc(s_ouse, 1)

            def waited(s, value):
                pool.wait_ge(s, value)
                pool.sem_inc(s_seen, 1)

            def over_sums(it, u):
                waited(s_rinv, it * UNROLL + (u + 1))
                nc.gpsimd.tensor_tensor(out=o_norm[:, :, :, :].rearrange("p t c d -> p (t c) d"),
                                        in0=o_tr[:, :, :, 0:2 * DH].rearrange("p t c d -> p (t c) d"),
                                        in1=rinv[:, :, :].rearrange("p t c -> p (t c)").unsqueeze(2).broadcast_to([P, NT * MAPS, 2 * DH]),
                                        op=ALU.mult).then_inc(s_ochain, 1)

            def weigh_second(it, u):
                waited(s_ochain, it * (UNROLL * 3) + (3 * u + 1))
                pool.sem_inc(s_ouse, 1)
                lam = nlam[:, bass.ds(it * UNROLL + u, 1), :].rearrange("p a h -> p (a h)")
                for h in range(2):
                    last = nc.gpsimd.tensor_tensor(out=o_two[:, :, h, :], in0=o_norm[:, :, 2 * h + 1, :],
                                                   in1=lam[:, h:h + 1].unsqueeze(1).broadcast_to([P, NT, 2 * DH]), op=ALU.mult)
                last.then_inc(s_ochain, 1)

            def add_maps(it, u):
                waited(s_ochain, it * (UNROLL * 3) + (3 * u + 2))
                nc.gpsimd.tensor_tensor(out=o_all[:, bass.ds(it * UNROLL + u, 1), :, :, :].rearrange("p a t h d -> p (a t) h d"),
                                        in0=o_norm[:, :, 0:MAPS:2, :], in1=o_two[:, :, :, :], op=ALU.add).then_inc(s_ochain, 1)

            def body(it, u, n):
                nb, first = it * (UNROLL * N_B), b_before(n) - (n - u) * N_B
                for s in range(NT):
                    slot = (u * NT + s) % NSLOT
                    if has_diagonal(s, n):
                        waited(s_bfree, nb + (NRING + first + b_before(n, s) - b_before(n) + 1))
                        diagonal = rest[:, (u * NT + s) % NDIAG, :].rearrange("p (c k) -> p c k", c=MAPS)
                        nc.gpsimd.affine_select(out=diagonal, in_=diagonal, compare_op=ALU.is_ge, fill=-1.0e30, base=0,
                                                pattern=[[0, MAPS], [-1, P]], channel_multiplier=1).then_inc(s_dmask, 1)
                    waited(s_bfree, nb + (NRING + first + b_before(n, s + 1) - b_before(n)))
                    nc.gpsimd.affine_select(out=probs[slot][:, :, 0:P], in_=probs[slot][:, :, 0:P], compare_op=ALU.is_ge,
                                            fill=0.0, base=0, pattern=[[0, MAPS], [1, P]],
                                            channel_multiplier=-1).then_inc(s_mask, 1)
                    if s == O_STEP + 1:
                        over_sums(it, u)
                    if s == O_STEP + 2:
                        weigh_second(it, u)
                    if s == O_STEP + 3:
                        add_maps(it, u)
                    if s == O_STEP + 4 and n + 1 < G:
                        nxt = it * UNROLL + (u + 1)
                        nc.gpsimd.tensor_copy(v_grp[:, (u + 1) % NBUF, :, :, 0:2 * DH].rearrange("p h t d -> p (h t) d"),
                                              v_all[:, bass.ds(nxt, 1), :, :, :].rearrange("p a h t d -> p (a h t) d")).then_inc(s_vgrp, 1)

            body(0, 0, 0)
            with pool.Fori(0, LOOPS) as it:
                for u in range(1, UNROLL + 1):
                    body(it, u, u)
            for n in range(1 + LOOPS * UNROLL, G):
                body((n - 1) // UNROLL, (n - 1) % UNROLL + 1, n)
            for stage in (over_sums, weigh_second, add_maps):
                stage(G // UNROLL, G % UNROLL)

        @block.scalar
        def _(act):
            nc.scalar.dma_start(wk[:, :], WkT).then_inc(s_x, 16)
            nc.scalar.dma_start(ident[:, :], c_ident).then_inc(s_masks, 16)
            nc.scalar.dma_start(causalf[:, :], c_causal).then_inc(s_masks, 16)
            for m, v in enumerate((lq1, lk1, lq2, lk2)):
                nc.scalar.dma_start(lvec[:, m, :, :].rearrange("p h d -> p (h d)"),
                                    v.rearrange("(a h) d -> a (h d)", a=1).partition_broadcast(P)).then_inc(s_lam, 16)

            def mid(u):
                act.wait_ge(s_rest, u + 1)
                nc.scalar.activation(part_sb[u][:, 1, :], rest[:, u % 2, :], ACT.Copy).then_inc(s_mid, 1)

            for u in range(N_EARLY_QK):
                act.wait_ge(s_proj, u + 1)
                nc.scalar.activation(part_sb[u][:, 0, :], bank[3 + u % PROJ_BANKS][:, :], ACT.Copy).then_inc(s_hi, 1)
                if u >= 1:
                    mid(u - 1)
            mid(N_EARLY_QK - 1)

            def block_mid(k):
                act.wait_ge(s_brest, k + 1)
                nc.scalar.activation(part_sb[N_EARLY_QK + k][:, 1, :], block_sb[:, k % 6, :], ACT.Copy).then_inc(s_bmid, 1)

            for u in range(N_EARLY_QK, N_QK):
                k = u - N_EARLY_QK
                act.wait_ge(s_proj, u + 1)
                if k >= 6:
                    act.wait_ge(s_blo, k - 5)
                nc.scalar.activation(block_sb[:, k % 6, :], bank[3 + u % PROJ_BANKS][:, :], ACT.Copy)
                nc.scalar.activation(part_sb[u][:, 0, :], bank[3 + u % PROJ_BANKS][:, :], ACT.Copy).then_inc(s_block, 1)
                if k >= 1:
                    block_mid(k - 1)
                if k == 0:
                    act.wait_ge(s_const, 5)
                    nc.scalar.activation(lexp[:, :, :], lsum[:, :, :], ACT.Exp).then_inc(s_lexp, 1)
            block_mid(N_QK - N_EARLY_QK - 1)
            for t in range(TT):
                act.wait_ge(s_vproj, t + 1)
                b, i = t // NT, t % NT
                nc.scalar.activation(v_all[:, b * GB:(b + 1) * GB, :, i, :],
                                     bank[3 + (N_QK + t) % PROJ_BANKS][:, 0:2 * DH * H].rearrange("p (g h d) -> p g h d", g=GB, h=2),
                                     ACT.Copy).then_inc(s_vcopy, 1)
            act.sem_inc(s_bfree, NRING)
            act.sem_inc(s_ocopy, 2)
            act.wait_ge(s_stored, N_QK * 16)

            def copy_out(it, u):
                act.wait_ge(s_pfree, it * (UNROLL * NT) + (NSLOT + (u + 1) * NT))
                for half in range(2):
                    nc.scalar.activation(oT[:, half * BANK:(half + 1) * BANK], pv[half][:, :], ACT.Copy).then_inc(s_ocopy, 1)

            def out_transposed(it, u, half, idx):
                act.wait_ge(s_bfill, it * (UNROLL * N_B) + (idx + 1))
                nc.scalar.activation(o_tr[:, 4 * half:4 * half + 4, :, :].rearrange("p t c d -> p (t c d)"), ring_b[idx % NRING][:, :],
                                     ACT.Copy).then_inc(s_bfree, 1)

            def body(it, u, n):
                nb, n8, first = it * (UNROLL * N_B), it * (UNROLL * NT), b_before(n) - (n - u) * N_B
                for s in range(NT):
                    slot = (u * NT + s) % NSLOT
                    act.wait_ge(s_pfree, n8 + (u * NT + s + 1))
                    for k, (kind, what) in enumerate(b_items(s, n)):
                        idx = first + b_before(n, s) - b_before(n) + k
                        if kind == "diagonal":
                            act.wait_ge(s_bfill, nb + (idx + 1))
                            if n or s >= NDIAG:
                                act.wait_ge(s_dused, n8 + (u * NT + s - NDIAG + 1))
                            nc.scalar.activation(rest[:, (u * NT + s) % NDIAG, :], ring_b[idx % NRING][:, :], ACT.Copy).then_inc(s_bfree, 1)
                            continue
                        if kind == "out":
                            if what == 0:
                                act.wait_ge(s_ouse, it * UNROLL + (u + 1))
                            out_transposed(it, u, what, idx)
                            continue
                        _, c, a, z = what
                        act.wait_ge(s_bfill, nb + (idx + 1))
                        nc.scalar.activation(probs[slot][:, c, a - P * s:z - P * s], ring_b[idx % NRING][:, 0:z - a],
                                             ACT.Exp, scale=SCALE).then_inc(s_bfree, 1)
                    if s == COPY_STEP and u >= 1:
                        copy_out(it, u - 1)

            body(0, 0, 0)
            with act.Fori(0, LOOPS) as it:
                for u in range(1, UNROLL + 1):
                    body(it, u, u)
            for n in range(1 + LOOPS * UNROLL, G):
                body((n - 1) // UNROLL, (n - 1) % UNROLL + 1, n)
            copy_out((G - 1) // UNROLL, (G - 1) % UNROLL)
            act.wait_ge(s_ouse, G + 1)
            for half in range(2):
                out_transposed(0, 0, half, b_before(G) + half)

            def exponentials(b):
                act.wait_ge(s_lgsub, b + 1)
                nc.scalar.activation(key[:, b * NT:(b + 1) * NT, :], pr[:, b * NT:(b + 1) * NT, :], ACT.Exp).then_inc(s_lgexp, 1)

            exponentials(0)
            for kind, i in late_order():
                if kind == "hidden":
                    b, e, f, q = i // (2 * HALF_Q * E), i // (2 * HALF_Q) % E, i // HALF_Q % 2, i % HALF_Q
                    act.wait_ge(s_hid, i + 1)
                    if (b, e) == (0, 6):
                        act.wait_ge(s_proj_o, QUADS)
                    if (b, e) == (0, 7):
                        act.wait_ge(s_oct, QUADS)
                    n0 = (b * HALF_Q + q) * BANK
                    nc.scalar.activation(hT[e][:, f, n0:n0 + BANK], bank[5 + i % 3][:, :], ACT.Gelu).then_inc(s_gelu, 1)
                elif kind == "heads":
                    act.wait_ge(s_oct, i + 1)
                    nc.scalar.activation(ocT[1][:, i % HALF_Q, 0:2, :, :].rearrange("p t a n -> p (t a n)"), bank[heads_bank(i)][:, :], ACT.Copy)
                    nc.scalar.activation(ocT[1][:, i % HALF_Q, 2:4, :, :].rearrange("p t a n -> p (t a n)"), bank[heads_bank(i) + 1][:, :],
                                         ACT.Copy).then_inc(s_octc, 1)
                elif kind == "x1":
                    act.wait_ge(s_x1t, i + 1)
                    nc.scalar.activation(xT[:, i * BANK:(i + 1) * BANK], bank[x1_bank(i)][:, :], ACT.Copy).then_inc(s_x1tc, 1)
                elif kind == "exp":
                    exponentials(i)
            for q in range(QUADS):
                act.wait_ge(s_var, q + 1)
                nc.scalar.activation(rstd[:, 4 * q:4 * q + 4], rstd[:, 4 * q:4 * q + 4], ACT.Sqrt).then_inc(s_std, 1)

        @block.vector
        def _(dve):
            nc.vector.memset(arena[64:P, 0:NBUF * nq // 2], 0.0).then_inc(s_const, 1)
            nc.vector.memset(oT[:, :], 1.0)
            nc.vector.memset(nlam[:, 0:1, :], 1.0)
            nc.vector.memset(m_parts[:, :, :], 0.0)
            nc.vector.memset(m_raw[:, :, :, :], -3.0e38).then_inc(s_const, 1)
            def low(u):
                dve.wait_ge(s_mid, u + 1)
                nc.vector.tensor_tensor(out=part_sb[u][:, 2, :], in0=rest[:, u % 2, :], in1=part_sb[u][:, 1, :],
                                        op=ALU.subtract).then_inc(s_lo, 1)

            for u in range(N_EARLY_QK):
                dve.wait_ge(s_hi, u + 1)
                if u >= 2:
                    dve.wait_ge(s_lo, u - 1)
                nc.vector.tensor_tensor(out=rest[:, u % 2, :], in0=bank[3 + u % PROJ_BANKS][:, :], in1=part_sb[u][:, 0, :],
                                        op=ALU.subtract).then_inc(s_rest, 1)
                if u >= 1:
                    low(u - 1)
            low(N_EARLY_QK - 1)
            dve.wait_ge(s_masks, 16 * 2)
            nc.vector.tensor_copy(identb[:, :], ident[:, :])
            nc.vector.tensor_copy(causalb[:, :], causalf[:, :]).then_inc(s_const, 1)
            dve.wait_ge(s_lam, 16 * 4)
            nc.vector.tensor_tensor(out=lprod[:, :, :, :], in0=lvec[:, 0:4:2, :, :], in1=lvec[:, 1:4:2, :, :], op=ALU.mult).then_inc(s_const, 1)
            dve.wait_ge(s_const, 4)
            nc.vector.tensor_reduce(out=lsum[:, :, :], in_=lprod[:, :, :, :], axis=AX.X, op=ALU.add).then_inc(s_const, 1)
            dve.wait_ge(s_lexp, 1)
            for b in range(B):
                nc.vector.scalar_tensor_tensor(out=nlam[:, 1 + b * GB:1 + (b + 1) * GB, :].rearrange("p g h -> p (g h)"),
                                               in0=lexp[:, 1, :], scalar=-LAMBDA_INIT, in1=lexp[:, 0, :],
                                               op0=ALU.add, op1=ALU.subtract).then_inc(s_const, 1)
            dve.wait_ge(s_const, 7)

            def take_max(unit, src):
                i, n, c0, c1, a, z = unit
                w = z - a
                return nc.vector.tensor_reduce(out=m_raw[:, c0:c1, i, n], in_=src[:, 0:(c1 - c0) * w].rearrange("p (c k) -> p c k", k=w),
                                               axis=AX.X, op=ALU.max)

            def split_max(a_done, chain, d_done=None):
                dve.wait_ge(s_afree, a_done)
                if d_done is not None:
                    dve.wait_ge(s_dused, d_done)
                nc.vector.tensor_reduce(out=m_neg[:, :], in_=m_raw[:, :, :, :].rearrange("p c t n -> p (c t) n"),
                                        axis=AX.X, op=ALU.max, negate=True).then_inc(s_mchain, 1)
                dve.wait_ge(s_mchain, chain + 1)
                nc.vector.tensor_copy(m_parts[:, 0, :], m_neg[:, :]).then_inc(s_mchain, 1)
                dve.wait_ge(s_mchain, chain + 2)
                nc.vector.tensor_tensor(out=m_parts[:, 1, :], in0=m_neg[:, :], in1=m_parts[:, 0, :],
                                        op=ALU.subtract).then_inc(s_mchain, 1)

            def copy_shift(idx, shifts):
                dve.wait_ge(s_shift, shifts)
                nc.vector.tensor_copy(mT[:, :], ring_a[idx % NRING][:, :].bitcast(BF16)[0:2 * MAPS * NT, 0:P]).then_inc(s_afree, 1)

            def invert_sums(it, u, b_done):
                dve.wait_ge(s_bfree, b_done)
                nc.vector.reciprocal(rinv[:, :, :], o_tr[:, :, :, 2 * DH]).then_inc(s_rinv, 1)

            idx = 0
            for unit in FIRST_UNITS:
                dve.wait_ge(s_afill, idx + 1)
                take_max(unit, ring_a[idx % NRING]).then_inc(s_afree, 1)
                idx += 1
            split_max(idx, 0)
            for k, unit in enumerate(EARLY_UNITS):
                if k == SHIFT_LAG:
                    dve.wait_ge(s_afill, idx + 1)
                    nc.vector.tensor_copy(mT[:, :], ring_a[idx % NRING][:, :].bitcast(BF16)[0:2 * MAPS * NT, 0:P]).then_inc(s_afree, 1)
                    idx += 1
                dve.wait_ge(s_afill, idx + 1)
                take_max(unit, ring_a[idx % NRING]).then_inc(s_afree, 1)
                idx += 1

            def body(it, u, n):
                na, n8 = it * (UNROLL * N_A), it * (UNROLL * NT)
                a = a_before(n) - (n - u) * N_A
                items = pe_order(n)[1]
                last_max = max((k for k, (kind, _) in enumerate(items) if kind == "max"), default=-1)
                outs = it * (UNROLL * N_B) + (b_before(n, O_STEP + 1) - (n - u) * N_B + NRING)
                for k, (kind, what) in enumerate(items):
                    if kind == "diagonal":
                        dve.wait_ge(s_dmask, n8 + (u * NT + what + 1))
                        take_max(diagonal_unit(DIAGONALS[what]), rest[:, (u * NT + what) % NDIAG, :]).then_inc(s_dused, 1)
                        if what == INVERT_AFTER:
                            invert_sums(it, u, outs)
                        continue
                    dve.wait_ge(s_afill, na + (a + 1))
                    if kind == "shift":
                        copy_shift(a, it * (UNROLL * 32) + 32 * (u + 1))
                    else:
                        take_max(what, ring_a[a % NRING]).then_inc(s_afree, 1)
                    a += 1
                    if k == last_max:
                        split_max(na + a, it * (UNROLL * 3) + 3 * (u + 1), n8 + (u * NT + len(MAX_FIRST)))
                if ("diagonal", INVERT_AFTER) not in items:
                    invert_sums(it, u, outs)

            body(0, 0, 0)
            with dve.Fori(0, LOOPS) as it:
                for u in range(1, UNROLL + 1):
                    body(it, u, u)
            for n in range(1 + LOOPS * UNROLL, G - 1):
                body((n - 1) // UNROLL, (n - 1) % UNROLL + 1, n)

            chain = [0]

            def link(ins):
                chain[0] += 1
                ins.then_inc(s_dchain, 1)
                dve.wait_ge(s_dchain, chain[0])

            V = nc.vector

            def invert_root(x, n):
                g, s = guess[:, 0:n], step[:, 0:n]
                link(V.tensor_scalar(g.bitcast(I32), x.bitcast(I32), 1, None, ALU.logical_shift_right))
                link(V.tensor_scalar(g.bitcast(I32), g.bitcast(I32), -1.0, float(0x5F3759DF), ALU.mult, ALU.add))
                for k in range(3):
                    link(V.scalar_tensor_tensor(out=s, in0=g, scalar=-0.5, in1=g, op0=ALU.mult, op1=ALU.mult))
                    link(V.tensor_tensor(out=s, in0=s, in1=x, op=ALU.mult))
                    link(V.scalar_tensor_tensor(out=x if k == 2 else g, in0=s, scalar=1.5, in1=g, op0=ALU.add, op1=ALU.mult))

            def squares(g0, g1):
                b = g0 // GB
                n = (g1 - g0) * NT * 2
                at = sq_at[b] + (g0 - b * GB) * NT * 2 * 2 * DH
                sq = arena[:, at:at + n * 2 * DH].rearrange("p (n d) -> p n d", d=2 * DH)
                flat = o_all[:, 1 + g0:1 + g1, :, :, :].rearrange("p g t h d -> p (g t h) d")
                link(V.tensor_tensor(out=sq, in0=flat, in1=flat, op=ALU.mult))
                link(V.tensor_reduce(out=ss[:, g0 * NT * 2:g1 * NT * 2], in_=sq, axis=AX.X, op=ALU.add))

            def normalise_heads(b):
                n = GB * NT * 2
                ssb = ss[:, b * n:(b + 1) * n]
                link(V.tensor_scalar(ssb, ssb, 1.0 / (2 * DH), EPS, ALU.mult, ALU.add))
                invert_root(ssb, n)
                inv = ssb.rearrange("p (g t h) -> p g t h", g=GB, t=NT)
                for h in range(2):
                    last = V.tensor_tensor(out=o_tok[b][:, :, :, h, :].rearrange("p t g d -> p g t d"),
                                           in0=o_all[:, 1 + b * GB:1 + (b + 1) * GB, :, h, :],
                                           in1=inv[:, :, :, h].unsqueeze(3).broadcast_to([P, GB, NT, 2 * DH]), op=ALU.mult)
                last.then_inc(s_onorm, 1)

            def quad_stats(x, q):
                for t in range(4 * q, 4 * q + 4):
                    last = V.bn_stats(stats[:, t, :], x[:, t, :])
                link(last)
                for t in range(4 * q, 4 * q + 4):
                    last = V.bn_aggr(mv[:, t, :], stats[:, t, :])
                link(last)
                return V.tensor_scalar(rstd[:, 4 * q:4 * q + 4], mv[:, 4 * q:4 * q + 4, 1], EPS, None, ALU.add)

            def quad_normalised(x, q):
                for t in range(4 * q, 4 * q + 4):
                    last = V.tensor_scalar(x[:, t, :], x[:, t, :], mv[:, t, 0:1], rstd[:, t:t + 1], ALU.subtract, ALU.mult)
                return last

            def residual(q):
                dve.wait_ge(s_proj_o, q + 1)
                xq = x_tok[:, 4 * q:4 * q + 4, :].rearrange("p t d -> p (t d)")
                V.tensor_tensor(out=xq, in0=bank[project_bank(q)][:, :], in1=xq, op=ALU.add).then_inc(s_x1sum, 1)
                dve.wait_ge(s_x1sum, q + 1)
                link(quad_stats(x_tok, q))

            def first_layernorm(b):
                invert_root(rstd[:, b * NT:(b + 1) * NT], NT)
                for q in range(b * HALF_Q, (b + 1) * HALF_Q):
                    quad_normalised(x_tok, q).then_inc(s_x1, 1)

            def router_logits(b):
                tiles = slice(b * NT, (b + 1) * NT)
                dve.wait_ge(s_logit, (b + 1) * HALF_Q)
                at = b * NT * E
                link(V.tensor_copy(lg[:, tiles, :], bank[logits_bank(b * HALF_Q)][:, at:at + NT * E].rearrange("p (t e) -> p t e", e=E)))
                link(V.tensor_reduce(out=rt1[:, tiles], in_=lg[:, tiles, :], axis=AX.X, op=ALU.max))
                V.tensor_tensor(out=pr[:, tiles, :], in0=lg[:, tiles, :], in1=rt1[:, tiles].unsqueeze(2).broadcast_to([P, NT, E]),
                                op=ALU.subtract).then_inc(s_lgsub, 1)

            dve.wait_ge(s_w, 16 * N_SMALL)
            link(V.tensor_scalar(wo[:, :, :], wo[:, :, :], rmscol[:, 0:1], 1.0 - LAMBDA_INIT, ALU.mult, ALU.mult))
            dve.wait_ge(s_ochain, 3 * (GB + 1))
            dve.wait_ge(s_bfree, NRING + b_before(G - 2))
            squares(0, GB)
            normalise_heads(0)
            body((G - 2) // UNROLL, (G - 2) % UNROLL + 1, G - 1)
            for q in range(HALF_Q):
                dve.wait_ge(s_oct, q + 1)
                for k in range(2):
                    last = V.tensor_copy(ocT[0][:, q, 2 * k:2 * k + 2, :, :].rearrange("p t a n -> p (t a n)"), bank[heads_bank(q) + k][:, :])
                last.then_inc(s_octc, 1)
            for q in range(HALF_Q):
                residual(q)
            first_layernorm(0)
            dve.wait_ge(s_vgrp, G)
            dve.wait_ge(s_ochain, 3 * (G - 1))
            squares(GB, G - 2)
            for q in range(HALF_Q):
                dve.wait_ge(s_x1t, q + 1)
                V.tensor_copy(xT[:, q * BANK:(q + 1) * BANK], bank[x1_bank(q)][:, :]).then_inc(s_x1tc, 1)
            router_logits(0)
            invert_sums(G // UNROLL, G % UNROLL, b_before(G) + 2 + NRING)

            dve.wait_ge(s_ochain, 3 * (G + 1))
            squares(G - 2, G)
            normalise_heads(1)
            for q in range(HALF_Q, QUADS):
                residual(q)
            first_layernorm(1)
            router_logits(1)

            def wide(x):
                return x.unsqueeze(2).broadcast_to([P, TT, E])

            dve.wait_ge(s_lgexp, B)
            link(V.tensor_reduce(out=rt2[:, :], in_=key[:, :, :], axis=AX.X, op=ALU.add))
            link(V.reciprocal(rt2[:, :], rt2[:, :]))
            V.tensor_tensor(out=pr[:, :, :], in0=key[:, :, :], in1=wide(rt2[:, :]), op=ALU.mult).then_inc(s_prob, 1)
            V.memset(ones[:, :], 1.0)
            V.tensor_copy(cand[:, :], change[:, 0, :])
            dve.wait_ge(s_prt, 1)
            link(V.tensor_copy(prT[:, :], bank[0][:, 0:P]))
            for k in range(SEARCH):
                for j in range(3):
                    last = V.tensor_scalar(cmp[:, j, :], prT[:, :], cand[:, j:j + 1].bitcast(F32), None, ALU.is_ge, ALU.add,
                                           accum_out=cnt[:, j:j + 1])
                last.then_inc(s_count, 1)
                dve.wait_ge(s_total, k + 1)
                link(V.scalar_tensor_tensor(out=met[:, :], in0=bank[1][:, 0:3], scalar=float(CAP), in1=weight[:, k, :],
                                            op0=ALU.is_ge, op1=ALU.mult))
                link(V.scalar_tensor_tensor(out=bits[:, :], in0=met[:, 0:1], scalar=met[:, 1:2], in1=met[:, 2:3],
                                            op0=ALU.bitwise_xor, op1=ALU.bitwise_xor))
                link(V.scalar_tensor_tensor(out=cand[:, :], in0=cand[:, :], scalar=bits[:, 0:1], in1=change[:, k + 1, :],
                                            op0=ALU.bitwise_xor, op1=ALU.bitwise_xor))
            threshold = cand[:, 0:1].bitcast(F32)
            link(V.tensor_scalar(cmp[:, 0, :], prT[:, :], threshold, None, ALU.is_gt, ALU.add, accum_out=cnt[:, 0:1]))
            V.tensor_scalar(cmp2[:, :], prT[:, :], threshold, None, ALU.is_equal, ALU.add, accum_out=cnt[:, 1:2]).then_inc(s_tie, 1)
            dve.wait_ge(s_tie, 1)
            link(V.tensor_tensor_scan(out=scan[:, :], data0=ones[:, :], data1=cmp2[:, :], initial=0.0, op0=ALU.mult, op1=ALU.add))
            dve.wait_ge(s_tiesum, 1)
            link(V.tensor_scalar(need[:, :], bank[1][:, 8:9], -1.0, float(CAP), ALU.mult, ALU.add))
            link(V.tensor_tensor(out=need[:, :], in0=need[:, :], in1=bank[1][:, 16:17], op=ALU.subtract))
            link(V.scalar_tensor_tensor(out=cmp2[:, :], in0=scan[:, :], scalar=need[:, 0:1], in1=cmp2[:, :],
                                        op0=ALU.is_le, op1=ALU.mult))
            V.tensor_tensor(out=selT[:, :], in0=cmp[:, 0, :], in1=cmp2[:, :], op=ALU.add).then_inc(s_selt, 1)
            dve.wait_ge(s_sel, 1)
            link(V.tensor_copy(sel[:, :, :], bank[2][:, 0:P].rearrange("p (t e) -> p t e", e=E)))
            link(V.tensor_reduce(out=rt1[:, :], in_=sel[:, :, :], axis=AX.X, op=ALU.max))
            link(V.tensor_scalar(rt1[:, :], rt1[:, :], -1.0, 1.0, ALU.mult, ALU.add))
            link(V.tensor_tensor(out=sel[:, :, :], in0=sel[:, :, :], in1=wide(rt1[:, :]), op=ALU.add))
            link(V.tensor_tensor(out=key[:, :, :], in0=pr[:, :, :], in1=sel[:, :, :], op=ALU.mult))
            link(V.scalar_tensor_tensor(out=key[:, :, :], in0=sel[:, :, :], scalar=-1.0, in1=key[:, :, :],
                                        op0=ALU.add, op1=ALU.add))
            link(V.tensor_reduce(out=rt2[:, :], in_=key[:, :, :], axis=AX.X, op=ALU.max))
            link(V.tensor_tensor(out=hit[:, :, :], in0=key[:, :, :], in1=wide(rt2[:, :]), op=ALU.is_equal))
            dve.wait_ge(s_pool_const, 3 + E)
            link(V.tensor_tensor(out=hit[:, :, :], in0=hit[:, :, :], in1=order[:, :].unsqueeze(1).broadcast_to([P, TT, E]),
                                 op=ALU.mult))
            link(V.tensor_reduce(out=rt1[:, :], in_=hit[:, :, :], axis=AX.X, op=ALU.max))
            link(V.tensor_tensor(out=hit[:, :, :], in0=hit[:, :, :], in1=wide(rt1[:, :]), op=ALU.is_equal))
            V.tensor_tensor(out=gate[:, :, :], in0=hit[:, :, :], in1=pr[:, :, :], op=ALU.mult).then_inc(s_gate, 1)
            dve.wait_ge(s_gate, 1)
            for q in range(QUADS):
                for e in range(E):
                    i = q * E + e
                    dve.wait_ge(s_y, i + 1)
                    if e >= 1:
                        dve.wait_ge(s_yacc, i)
                    for t in range(4 * q, 4 * q + 4):
                        last = V.scalar_tensor_tensor(out=y[:, t, :], in0=bank[Y_BANKS[i % len(Y_BANKS)]][:, (t % 4) * D:(t % 4 + 1) * D],
                                                      scalar=gate[:, t, e:e + 1], in1=(y if e else x_tok)[:, t, :],
                                                      op0=ALU.mult, op1=ALU.add)
                    last.then_inc(s_yacc, 1)
                dve.wait_ge(s_yacc, (q + 1) * E)
                quad_stats(y, q).then_inc(s_var, 1)
                dve.wait_ge(s_std, q + 1)
                link(V.reciprocal(rstd[:, 4 * q:4 * q + 4], rstd[:, 4 * q:4 * q + 4]))
                quad_normalised(y, q).then_inc(s_final, 1)

        @block.tensor
        def _(pe):
            def projection(i):
                dst, last = bank[3 + i % PROJ_BANKS], i - PROJ_BANKS
                if 0 <= last < N_EARLY_QK:
                    pe.wait_ge(s_rest, last + 1)
                elif N_EARLY_QK <= last < N_QK:
                    pe.wait_ge(s_block, last - N_EARLY_QK + 1)
                elif last >= N_QK:
                    pe.wait_ge(s_vcopy, last - N_QK + 1)
                if i < N_QK:
                    b, half, w, t0 = i // 8, i // 4 % 2, (wq, wk)[i // 2 % 2], i % 2 * BANK
                    nc.tensor.matmul(dst[:, :], w[:, half * P:(half + 1) * P],
                                     xT[:, b * N + t0:b * N + t0 + BANK], start=True, stop=True).then_inc(s_proj, 1)
                else:
                    t = i - N_QK
                    nc.tensor.matmul(dst[:, 0:2 * DH * H], xT[:, t * P:(t + 1) * P], wv[:, :],
                                     start=True, stop=True).then_inc(s_vproj, 1)

            pe.wait_ge(s_x, 16 * 4)
            for i in range(PROJ_FIRST - 1):
                projection(i)
            pe.wait_ge(s_x2, 16 * 2)
            projection(PROJ_FIRST - 1)

            def max_unit(buf, unit, dst, masked=False):
                i, n, c0, c1, a, z = unit
                for c in range(c0, c1):
                    at = (c - c0) * (z - a)
                    last = nc.tensor.matmul(dst[:, at:at + z - a], q_op[buf][:, c, i * P:(i + 1) * P], k_op[buf][:, c, a:z],
                                            start=True, stop=not masked)
                    if masked:
                        last = nc.tensor.matmul(dst[:, at:at + P], identb[:, :], causalb[:, :], start=False, stop=True)
                return last

            def shift_unit(idx, chain, free):
                pe.wait_ge(s_mchain, chain)
                pe.wait_ge(s_afree, free)
                nc.tensor.transpose(ring_a[idx % NRING][:, :].bitcast(BF16)[:, 0:P],
                                    m_parts[:, :, :].rearrange("p r n -> p (r n)"), identb[:, :]).then_inc(s_afill, 1)

            def out_unit(half, idx, free):
                pe.wait_ge(s_bfree, free)
                for t in range(4):
                    last = nc.tensor.transpose(ring_b[idx % NRING][:, t * P:(t + 1) * P],
                                               oT[:, half * BANK + t * P:half * BANK + (t + 1) * P], ident[:, :])
                last.then_inc(s_bfill, 1)

            pe.wait_ge(s_const, 3)
            pe.wait_ge(s_load[0], LOAD_INC)
            first = [(0, x) for x in FIRST_UNITS] + [(1, x) for x in EARLY_UNITS]
            first.insert(len(FIRST_UNITS) + SHIFT_LAG, (None, None))
            i = PROJ_FIRST
            for idx, (buf, unit) in enumerate(first):
                if buf is None:
                    shift_unit(idx, 3, idx - 2)
                else:
                    if idx == len(FIRST_UNITS):
                        pe.wait_ge(s_load[1], LOAD_INC)
                    if idx >= NRING:
                        pe.wait_ge(s_afree, idx - 2)
                    max_unit(buf, unit, ring_a[idx % NRING], masked=unit[1] == 2).then_inc(s_afill, 1)
                if idx % 2 and i < N_PROJ:
                    projection(i)
                    i += 1
            for i in range(i, N_PROJ):
                projection(i)
            pe.wait_ge(s_vcopy, TT)

            def products(it, t, span):
                n8, u, s = it * (UNROLL * NT), t // NT, t % NT
                if s == 0:
                    pe.wait_ge(s_vgrp, it * UNROLL + (u + 1))
                    pe.wait_ge(s_ocopy, it * (UNROLL * 2) + 2 * (u + 1))
                pe.wait_ge(s_mask, n8 + (t + 1))
                a, z = span
                half = a // BANK
                for c in range(MAPS):
                    last = nc.tensor.matmul(pv[half][32 * c:32 * c + 32, a - half * BANK:z - half * BANK],
                                            v_grp[:, u % NBUF, c // 2, s, :],
                                            probs[t % NSLOT][:, c, a - P * s:z - P * s],
                                            start=s == 0, stop=s == (3 if half == 0 else 7))
                if z == N:
                    last.then_inc(s_pfree, 1)

            def heads(q):
                pe.wait_ge(s_onorm, q // HALF_Q + 1)
                if 1 <= q < HALF_Q:
                    pe.wait_ge(s_octc, q)
                for t in range(4):
                    for a in range(2):
                        last = nc.tensor.transpose(bank[heads_bank(q) + t // 2][:, (t % 2 * 2 + a) * P:(t % 2 * 2 + a + 1) * P],
                                                   o_tok[q // HALF_Q][:, 4 * (q % HALF_Q) + t, 4 * a:4 * a + 4, :, :].rearrange("p g h d -> p (g h d)"),
                                                   ident[:, :])
                last.then_inc(s_oct, 1)

            def project(q):
                pe.wait_ge(s_octc, q + 1)
                if q:
                    pe.wait_ge(s_x1sum, q)
                for t in range(4):
                    for a in range(2):
                        last = nc.tensor.matmul(bank[project_bank(q)][:, t * D:(t + 1) * D], ocT[q // HALF_Q][:, q % HALF_Q, t, a, :],
                                                wo[:, a, :], start=a == 0, stop=a == 1)
                last.then_inc(s_proj_o, 1)

            def x1_transposed(q):
                pe.wait_ge(s_x1, q + 1)
                for t in range(4):
                    last = nc.tensor.transpose(bank[x1_bank(q)][:, t * P:(t + 1) * P], x_tok[:, 4 * q + t, :], ident[:, :])
                last.then_inc(s_x1t, 1)

            def logits(q):
                pe.wait_ge(s_x1tc, q + 1)
                for t in range(4 * q, 4 * q + 4):
                    last = nc.tensor.matmul(bank[logits_bank(q)][:, t * E:(t + 1) * E], xT[:, t * P:(t + 1) * P], wg[:, :],
                                            start=True, stop=True)
                last.then_inc(s_logit, 1)

            to_logits = {"heads": heads, "project": project, "x1": x1_transposed, "logits": logits}

            def body(it, u, n):
                na, nb = it * (UNROLL * N_A), it * (UNROLL * N_B)
                a, b_idx = a_before(n) - (n - u) * N_A, b_before(n) - (n - u) * N_B
                between = list(FIRST_BATCH) if n == G - 1 else []
                pe.wait_ge(s_shift, it * (UNROLL * 32) + 32 * (u + 1))
                loaded = False
                order, _ = pe_order(n)
                for k, (where, kind, what) in enumerate(order):
                    while between and k >= between[0][0] * len(order):
                        _, name, q = between.pop(0)
                        to_logits[name](q)
                    if (kind == "early" or kind == "diagonal" and what >= len(MAX_FIRST)) and not loaded:
                        pe.wait_ge(s_load[(u + 2) % NBUF], it * LOAD_INC + ((u + 2) // NBUF + 1) * LOAD_INC)
                        loaded = True
                    if kind == "score":
                        s, c, lo, hi = what
                        pe.wait_ge(s_bfree, nb + (b_idx + 1))
                        nc.tensor.matmul(ring_b[b_idx % NRING][:, 0:hi - lo], k_op[u % NBUF][:, c, s * P:(s + 1) * P],
                                         q_op[u % NBUF][:, c, lo:hi], start=True, stop=True).then_inc(s_bfill, 1)
                        b_idx += 1
                    elif kind == "diagonal":
                        pe.wait_ge(s_bfree, nb + (b_idx + 1))
                        max_unit((u + (1 if what < len(MAX_FIRST) else 2)) % NBUF, diagonal_unit(DIAGONALS[what]),
                                 ring_b[b_idx % NRING]).then_inc(s_bfill, 1)
                        b_idx += 1
                    elif kind == "out":
                        out_unit(what, b_idx, nb + (b_idx + 1))
                        b_idx += 1
                    elif where == "products":
                        products(it, u * NT + kind, what)
                    elif kind == "shift":
                        shift_unit(a, it * (UNROLL * 3) + 3 * (u + 2), na + (a - 2))
                        a += 1
                    else:
                        pe.wait_ge(s_afree, na + (a - 2))
                        max_unit((u + (2 if kind == "early" else 1)) % NBUF, what, ring_a[a % NRING]).then_inc(s_afill, 1)
                        a += 1

            pe.sem_inc(s_pfree, NSLOT)
            body(0, 0, 0)
            with pe.Fori(0, LOOPS) as it:
                for u in range(1, UNROLL + 1):
                    body(it, u, u)
            for n in range(1 + LOOPS * UNROLL, G):
                body((n - 1) // UNROLL, (n - 1) % UNROLL + 1, n)
            for t in range(G * NT - LAG, G * NT):
                for span in spans(P * (t % NT), N):
                    products(0, t, span)
            pe.wait_ge(s_ocopy, 2 * (G + 1))
            for half in range(2):
                out_unit(half, b_before(G) + half, b_before(G) + half + 1)

            def hidden(i):
                b, e, f, q = i // (2 * HALF_Q * E), i // (2 * HALF_Q) % E, i // HALF_Q % 2, i % HALF_Q
                if i >= 3:
                    pe.wait_ge(s_gelu, i - 2)
                n0 = (b * HALF_Q + q) * BANK
                nc.tensor.matmul(bank[5 + i % 3][:, :], w1[:, e, f * P:(f + 1) * P], xT[:, n0:n0 + BANK],
                                 start=True, stop=True).then_inc(s_hid, 1)

            def expert_out(i):
                q, e = i // E, i % E
                if i % (HALF_Q * E) == 0:
                    pe.wait_ge(s_gelu, (q // HALF_Q + 1) * N_HID // B)
                if i >= len(Y_BANKS):
                    pe.wait_ge(s_yacc, i - len(Y_BANKS) + 1)
                elif Y_BANKS[i] >= 5:
                    pe.wait_ge(s_gelu, N_HID)
                dst = bank[Y_BANKS[i % len(Y_BANKS)]]
                for t in range(4):
                    for f in range(2):
                        last = nc.tensor.matmul(dst[:, t * D:(t + 1) * D], hT[e][:, f, (4 * q + t) * P:(4 * q + t + 1) * P],
                                                w2[:, e, f, :], start=f == 0, stop=f == 1)
                last.then_inc(s_y, 1)

            pe.wait_ge(s_bfree, NRING + b_before(G) + 2)
            for kind, i in late_order():
                if kind == "hidden":
                    hidden(i)
                elif kind in to_logits:
                    to_logits[kind](i)
                elif kind == "probs":
                    pe.wait_ge(s_prob, 1)
                    nc.tensor.transpose(bank[0][:, 0:P], pr[:, :, :].rearrange("p t e -> p (t e)"), ident[:, :]).then_inc(s_prt, 1)
                elif kind == "search":
                    pe.wait_ge(s_count, i + 1)
                    nc.tensor.matmul(bank[1][:, 0:3], same[:, :], cnt[:, 0:3], start=True, stop=True).then_inc(s_total, 1)
                elif kind == "ties":
                    pe.wait_ge(s_tie, 1)
                    nc.tensor.matmul(bank[1][:, 8:9], same[:, :], cnt[:, 0:1], start=True, stop=True)
                    nc.tensor.matmul(bank[1][:, 16:17], before[:, :], cnt[:, 1:2], start=True, stop=True).then_inc(s_tiesum, 1)
                elif kind == "y":
                    expert_out(i)
                elif kind == "picked":
                    pe.wait_ge(s_selt, 1)
                    nc.tensor.transpose(bank[2][:, 0:P], selT[:, :], ident[:, :]).then_inc(s_sel, 1)

            for i in range(Y_SOON, QUADS * E):
                expert_out(i)



_INS = ["X", "XT", "WqT", "WkT", "WvT", "WoT", "lq1", "lk1", "lq2", "lk2", "rms", "Wg", "W1", "W2",
        "c_ident", "c_causal", "c_same", "c_before", "c_weight", "c_step"]


def kernel(**inputs):
    import numpy as np
    import concourse.bacc as bacc
    from concourse.bass_utils import run_bass_kernel_spmd

    x = np.asarray(inputs["L0_attn_X"])
    arrays = {"X": x, "XT": x.reshape(T, D).T}
    for n in ("Wq", "Wk", "Wv", "Wo"):
        arrays[n + "T"] = np.asarray(inputs[f"L0_attn_{n}"]).T
    for n in ("WqT", "WkT"):
        arrays[n] = arrays[n].reshape(D, GB, MAPS, DH).transpose(0, 1, 3, 2).reshape(D, 2 * DH * H)
    for n in ("lq1", "lk1", "lq2", "lk2"):
        arrays[n] = inputs[f"L0_attn_{n}"]
    arrays["rms"] = inputs["L0_attn_rms_scale"]
    for n in ("Wg", "W1", "W2"):
        arrays[n] = inputs[f"L0_ffn_{n}"]
    p = np.arange(P)
    same_expert = (p[:, None] - p[None, :]) % E == 0
    arrays["c_ident"] = np.eye(P, dtype=np.float32)
    arrays["c_causal"] = np.where(p[None, :] > p[:, None], np.float32(-1e30), np.float32(0))
    arrays["c_same"] = same_expert.astype(np.float32)
    arrays["c_before"] = (same_expert & (p[:, None] < p[None, :])).astype(np.float32)

    low = np.array([1 << (N_BITS - 2 - 2 * k) for k in range(SEARCH)] + [0])
    arrays["c_weight"] = (low[:SEARCH, None] * np.array([1, 3, 1])).astype(np.float32)
    own = low[:, None] * np.array([1, 2, 3])
    arrays["c_step"] = np.concatenate([own[:1], own[:-1] ^ own[1:]]).astype(np.int32)

    nc = bacc.Bacc("TRN2", target_bir_lowering=False, num_devices=1)
    ins = {f"in_{n}": np.ascontiguousarray(arrays[n]) for n in _INS}
    args = [nc.dram_tensor(n, a.shape, mybir.dt.from_np(a.dtype), kind="ExternalInput").ap() for n, a in ins.items()]
    args.append(nc.dram_tensor("out", (B, N, D), F32, kind="ExternalOutput").ap())
    build(nc, *args)
    return run_bass_kernel_spmd(nc, [ins], core_ids=[0]).results[0]["out"]
```
